# Optimizing a Trainium2 kernel written in Bass

```python
import numpy as np
import jax
import jax.numpy as jnp

def _softmax(x, axis=-1):
    return jax.nn.softmax(x, axis=axis)

def _gelu(x):
    return jax.nn.gelu(x, approximate=True)

def _silu(x):
    return jax.nn.silu(x)

def _sigmoid(x):
    return jax.nn.sigmoid(x)

def _layernorm(x, axis=-1, eps=1e-05):
    m = jnp.mean(x, axis=axis, keepdims=True)
    v = jnp.var(x, axis=axis, keepdims=True)
    return (x - m) / jnp.sqrt(v + eps)

def _scatter_add(tgt, idx, src, axis=0):
    return tgt.at[idx].add(src)

def _segment_sum(src, seg, n):
    return jax.ops.segment_sum(src, seg, n)
kernel_name = 'mk_flamingo_gated_d1_seqx_r8_1554b9'

def setup_inputs(seed: int=0):
    np.random.seed(seed)
    _w = jnp.asarray

    def _rec_inputs():
        import jax
        import jax.numpy as jnp
        _rk = jax.random.key(seed)
        x = 7.22e-05 + 1 * jax.random.normal(jax.random.fold_in(_rk, 1), (64, 64, 256), jnp.float32)
        _lenS = 64 - jax.random.randint(jax.random.fold_in(_rk, 7), (64,), 0, max(1, 64 // 4) + 1, jnp.int32)
        _lenS2 = 64 - jax.random.randint(jax.random.fold_in(_rk, 8), (64,), 0, max(1, 64 // 4) + 1, jnp.int32)
        _ctx_2048P = jax.random.normal(jax.random.fold_in(_rk, 11), (64, 16, 256), jnp.float32)
        _ctx_2048c = jax.random.dirichlet(jax.random.fold_in(_rk, 511), 0.3 * jnp.ones((16,), jnp.float32), (64, 64))
        _ctx_2048t = jnp.einsum('bsk,bkd->bsd', _ctx_2048c, _ctx_2048P)
        _ctx_2048t = _ctx_2048t * jax.lax.rsqrt(jnp.mean(jnp.square(_ctx_2048t)) + 1e-12) * 0.953939
        ctx_2048 = 4.13588e-05 + 0.999923 * (_ctx_2048t + 0.3 * jax.random.normal(jax.random.fold_in(_rk, 611), (64, 64, 256), jnp.float32))
        _g = jax.random.normal(jax.random.fold_in(_rk, 9001), (2, 1), jnp.float32)
        _g = jnp.sign(_g) * jnp.maximum(jnp.abs(_g), 1.0) + (_g == 0) * 1.0
        g_xattn = _g[0]
        g_ffn = _g[1]
        return (x, ctx_2048, g_xattn, g_ffn)
    x, ctx_2048, g_xattn, g_ffn = _rec_inputs()

    def _L0_xattn_setup():
        import math
        import jax, jax.numpy as jnp
        import numpy as np
        HEADS = 16
        MASKED_BIAS = -10000.0

        def _mha(q, k, v):
            B, Sq, D = q.shape
            Sk = k.shape[-2]
            hd = D // HEADS
            qh = q.reshape(B, Sq, HEADS, hd).transpose(0, 2, 1, 3)
            kh = k.reshape(B, Sk, HEADS, hd).transpose(0, 2, 1, 3)
            vh = v.reshape(B, Sk, HEADS, hd).transpose(0, 2, 1, 3)
            scores = jnp.einsum('bhqd,bhkd->bhqk', qh, kh) / math.sqrt(hd)
            qi = jnp.arange(Sq)[:, None] + (Sk - Sq)
            ki = jnp.arange(Sk)[None, :]
            causal = ki <= qi
            scores = jnp.where(causal[None, None], scores, jnp.asarray(MASKED_BIAS, scores.dtype))
            attn = jax.nn.softmax(scores, axis=-1)
            out = jnp.einsum('bhqk,bhkd->bhqd', attn, vh)
            return out.transpose(0, 2, 1, 3).reshape(B, Sq, D)
        key = jax.random.key(seed)
        kq, kk, kv = jax.random.split(key, 3)
        B, S, D = (4, 128, 256)
        q = jax.random.normal(kq, (B, S, D), dtype=jnp.float32)
        k = jax.random.normal(kk, (B, S, D), dtype=jnp.float32)
        v = jax.random.normal(kv, (B, S, D), dtype=jnp.float32)
        return {'q': q, 'k': k, 'v': v}
    _L0_xattn_all = _L0_xattn_setup()
    _L0_xattn_in = {k: v for k, v in _L0_xattn_all.items() if k in ()}
    del _L0_xattn_all

    def _L0_ffn_setup():
        import jax, jax.numpy as jnp
        import numpy as np
        B, S, H = (2, 128, 256)
        E, F = (16, 128)
        TOP_K = 4
        SH_F = 704
        key = jax.random.key(seed)
        ks = jax.random.split(key, 9)
        sc = 0.02
        return {'hidden_states': jax.random.normal(ks[0], (B, S, H), dtype=jnp.float32), 'w_router': jax.random.normal(ks[1], (H, E), dtype=jnp.float32) * sc, 'w_gate': jax.random.normal(ks[2], (E, H, F), dtype=jnp.float32) * sc, 'w_up': jax.random.normal(ks[3], (E, H, F), dtype=jnp.float32) * sc, 'w_down': jax.random.normal(ks[4], (E, F, H), dtype=jnp.float32) * sc, 'w_sh_gate': jax.random.normal(ks[5], (H, SH_F), dtype=jnp.float32) * sc, 'w_sh_up': jax.random.normal(ks[6], (H, SH_F), dtype=jnp.float32) * sc, 'w_sh_down': jax.random.normal(ks[7], (SH_F, H), dtype=jnp.float32) * sc, 'w_sh_expert_gate': jax.random.normal(ks[8], (H, 1), dtype=jnp.float32) * sc}
    _L0_ffn_all = _L0_ffn_setup()
    _L0_ffn_in = {k: v for k, v in _L0_ffn_all.items() if k in ('w_router', 'w_gate', 'w_up', 'w_down', 'w_sh_gate', 'w_sh_up', 'w_sh_down', 'w_sh_expert_gate')}
    del _L0_ffn_all
    return {'x': x, 'ctx_2048': ctx_2048, 'g_xattn': g_xattn, 'g_ffn': g_ffn, 'L0_ffn_w_router': _L0_ffn_in['w_router'], 'L0_ffn_w_gate': _L0_ffn_in['w_gate'], 'L0_ffn_w_up': _L0_ffn_in['w_up'], 'L0_ffn_w_down': _L0_ffn_in['w_down'], 'L0_ffn_w_sh_gate': _L0_ffn_in['w_sh_gate'], 'L0_ffn_w_sh_up': _L0_ffn_in['w_sh_up'], 'L0_ffn_w_sh_down': _L0_ffn_in['w_sh_down'], 'L0_ffn_w_sh_expert_gate': _L0_ffn_in['w_sh_expert_gate']}

def reference(x, ctx_2048, g_xattn, g_ffn, L0_ffn_w_router, L0_ffn_w_gate, L0_ffn_w_up, L0_ffn_w_down, L0_ffn_w_sh_gate, L0_ffn_w_sh_up, L0_ffn_w_sh_down, L0_ffn_w_sh_expert_gate):
    import jax
    import jax.numpy as jnp

    def _L0_xattn_ref(q, k, v):
        import math
        import jax, jax.numpy as jnp
        import numpy as np
        HEADS = 16
        MASKED_BIAS = -10000.0

        def _mha(q, k, v):
            B, Sq, D = q.shape
            Sk = k.shape[-2]
            hd = D // HEADS
            qh = q.reshape(B, Sq, HEADS, hd).transpose(0, 2, 1, 3)
            kh = k.reshape(B, Sk, HEADS, hd).transpose(0, 2, 1, 3)
            vh = v.reshape(B, Sk, HEADS, hd).transpose(0, 2, 1, 3)
            scores = jnp.einsum('bhqd,bhkd->bhqk', qh, kh) / math.sqrt(hd)
            qi = jnp.arange(Sq)[:, None] + (Sk - Sq)
            ki = jnp.arange(Sk)[None, :]
            causal = ki <= qi
            scores = jnp.where(causal[None, None], scores, jnp.asarray(MASKED_BIAS, scores.dtype))
            attn = jax.nn.softmax(scores, axis=-1)
            out = jnp.einsum('bhqk,bhkd->bhqd', attn, vh)
            return out.transpose(0, 2, 1, 3).reshape(B, Sq, D)
        return _mha(q, k, v)

    def _L0_ffn_ref(hidden_states, w_router, w_gate, w_up, w_down, w_sh_gate, w_sh_up, w_sh_down, w_sh_expert_gate):
        import jax, jax.numpy as jnp
        import numpy as np
        B, S, H = (2, 128, 256)
        E, F = (16, 128)
        TOP_K = 4
        SH_F = 704
        b, s, h = hidden_states.shape
        x = hidden_states.reshape(-1, h)
        router_logits = x @ w_router
        probs = jax.nn.softmax(router_logits, axis=-1)
        topk_w, topk_ids = jax.lax.top_k(probs, TOP_K)
        topk_w = topk_w / jnp.sum(topk_w, axis=-1, keepdims=True)
        combine = jnp.sum(jax.nn.one_hot(topk_ids, E, dtype=x.dtype) * topk_w[..., None], axis=1)
        g = jnp.einsum('th,ehf->tef', x, w_gate)
        u = jnp.einsum('th,ehf->tef', x, w_up)
        act = jax.nn.silu(g) * u
        act = act * combine[:, :, None]
        moe_out = jnp.einsum('tef,efh->th', act, w_down)
        sg = jax.nn.silu(x @ w_sh_gate) * (x @ w_sh_up)
        shared = sg @ w_sh_down
        gate = jax.nn.sigmoid(x @ w_sh_expert_gate)
        out = moe_out + gate * shared
        return out.reshape(b, s, h)
    x = x + jnp.tanh(g_xattn[0]) * _L0_xattn_ref(_layernorm(x, axis=-1), ctx_2048, ctx_2048)
    x = x + jnp.tanh(g_ffn[0]) * _L0_ffn_ref(_layernorm(x, axis=-1), L0_ffn_w_router, L0_ffn_w_gate, L0_ffn_w_up, L0_ffn_w_down, L0_ffn_w_sh_gate, L0_ffn_w_sh_up, L0_ffn_w_sh_down, L0_ffn_w_sh_expert_gate)
    return x

_drawn_inputs = setup_inputs


def setup_inputs(seed=0):
    import zlib

    import numpy as np

    out = dict(_drawn_inputs(seed))
    spreads = {}
    factors = {'L0_ffn_w_router': 8.0,
     'L0_ffn_w_gate': 8.0,
     'L0_ffn_w_up': 8.0,
     'L0_ffn_w_down': 8.0,
     'L0_ffn_w_sh_gate': 5.229,
     'L0_ffn_w_sh_up': 5.178,
     'L0_ffn_w_sh_down': 5.191,
     'L0_ffn_w_sh_expert_gate': 8.0}
    for name, (base, spread) in spreads.items():
        noise = np.random.default_rng([zlib.crc32(name.encode()), seed]).standard_normal(out[name].shape)
        drawn = base * np.exp(spread * noise) if base else spread * noise
        out[name] = jnp.asarray(drawn.astype(out[name].dtype))
    for name, factor in factors.items():
        out[name] = (out[name] * factor).astype(out[name].dtype)
    return out
```

```python
import concourse.bass as bass
from concourse import mybir
from contextlib import ExitStack

D = 256
KC = D // 128
SEQ = 64
HEADS, HD = 16, 16
EXPERTS, TOP_K = 16, 4
SHARED = 704
SHARED_CHUNKS = -(-SHARED // 128)
SHARED_REST = SHARED - 128 * (SHARED_CHUNKS - 1)
CHUNKS = EXPERTS + SHARED_CHUNKS
PAIR = 2 * SEQ
PAIRS = 4
GROUP = PAIRS * PAIR
QUARTERS = 4
POINTS = 2 * CHUNKS
ROUTES = EXPERTS + 2
COMBINE = EXPERTS + 1
RING = 4
STAGING = 4
VCOLS = 2 * 2 * HD + 2
MASKED = -10000.0
EPS = 1e-5
FAR = 3.0e38

START = {"load": -8, "norm": -3, "transpose": 0, "score": 2, "turn": 5, "value": 6, "project": 8,
         "route": 10, "weigh": 12}


def stage_points():
    points = [[] for _ in range(POINTS)]
    for p in range(PAIRS):
        for name, offset in START.items():
            points[max(0, 9 * p + 1 + offset)].append((name, p))
    return points


STAGES = stage_points()


def known(eng, value):
    return value if isinstance(value, int) else eng.snap(eng.to_reg(value))


def after(eng, sem, count, apart=None):
    if apart is not None and not isinstance(count, int):
        count = known(eng, count)
        eng.wait_ge(*apart)
    if not isinstance(count, int) or count > 0:
        eng.wait_ge(sem, count)


def flamingo_block(nc, x, ctx_in, g_xattn, g_ffn, w_router, w_gate, w_up, w_down, w_sh_gate, w_sh_up,
                   w_sh_down, w_sh_expert_gate, out):
    f32, f32r, u8 = mybir.dt.float32, mybir.dt.float32r, mybir.dt.uint8
    ALU, ACT, AX = mybir.AluOpType, mybir.ActivationFunctionType, mybir.AxisListType

    tokens = x.shape[0] * x.shape[1]
    groups = tokens // GROUP
    x_rows = x.rearrange("b s d -> (b s) d")
    out_rows = out.rearrange("b s d -> (b s) d")
    combine_dram = nc.dram_tensor("combine_rows", (2, COMBINE, GROUP), f32, kind="Internal").ap()

    ctx = ExitStack()
    with ctx:
        def sb(name, shape, dt=f32):
            return ctx.enter_context(nc.sbuf_tensor(name, shape, dt))

        def ps(name, shape):
            return ctx.enter_context(nc.psum_tensor(name, shape, f32))

        def sem(name):
            return ctx.enter_context(nc.semaphore(name))

        wgu_hi = sb("wgu_hi", [128, CHUNKS, KC, 2, 128], f32r)
        wgu_lo = sb("wgu_lo", [128, CHUNKS, KC, 2, 128], f32r)
        wd_hi = sb("wd_hi", [128, CHUNKS, D], f32r)
        wd_lo = sb("wd_lo", [128, CHUNKS, D], f32r)
        wr_hi = sb("wr_hi", [128, KC, ROUTES], f32r)
        wr_lo = sb("wr_lo", [128, KC, ROUTES], f32r)
        wr_raw = sb("wr_raw", [128, KC, ROUTES])
        raw = sb("raw", [128, STAGING, 3 * D])
        ident = sb("ident", [128, 128])
        head_mask = sb("head_mask", [128, QUARTERS])
        head_two = sb("head_two", [128, 2, QUARTERS])
        causal_f = sb("causal_f", [128, SEQ])
        causal = sb("causal", [128, SEQ], u8)
        minus_half = sb("minus_half", [128, 1])
        gates = sb("gates", [128, 2])
        gate_tanh = sb("gate_tanh", [128, 2])
        x_in = sb("x_in", [128, 2, D])
        ctx_k = sb("ctx_k", [128, QUARTERS, 2, SEQ])
        stats = sb("stats", [128, 6])
        moments = sb("moments", [128, 2])
        rstd = sb("rstd", [128, 1])
        stats2 = sb("stats2", [128, 6])
        moments2 = sb("moments2", [128, 2])
        rstd2 = sb("rstd2", [128, 1])
        x_norm = sb("x_norm", [128, QUARTERS, 2, SEQ])
        q_t = sb("q_t", [128, QUARTERS, 128])
        k_t = sb("k_t", [128, QUARTERS, SEQ])
        k_block = sb("k_block", [128, QUARTERS, QUARTERS, SEQ])
        p_t = k_block[:, :, :, :].rearrange("p a b c -> p (a b c)").rearrange("p (j t) -> p j t", t=128)
        scores = sb("scores", [128, HEADS, SEQ])
        row_max = sb("row_max", [128, HEADS])
        probs = sb("probs", [128, HEADS, SEQ])
        v_block = sb("v_block", [128, HEADS // 2, VCOLS])
        inv_sum = sb("inv_sum", [128, HEADS])
        attended = sb("attended", [128, D])
        x2 = sb("x2", [128, 2, PAIRS, D])
        x2_norm = sb("x2_norm", [128, D])
        x2t_hi = sb("x2t_hi", [128, 2, KC, GROUP], f32r)
        x2t_lo = sb("x2t_lo", [128, 2, KC, GROUP], f32r)
        logits = sb("logits", [128, EXPERTS + 8 - TOP_K])
        top8 = sb("top8", [128, 8])
        top_k = sb("top_k", [128, 8])
        replaced = sb("replaced", [128, EXPERTS + 8 - TOP_K])
        exponent = sb("exponent", [128, COMBINE])
        exped = sb("exped", [128, COMBINE])
        chosen = sb("chosen", [128, EXPERTS])
        weighed = sb("weighed", [128, EXPERTS])
        sums = sb("sums", [128, 2])
        inv_sums = sb("inv_sums", [128, 2])
        combine = sb("combine", [128, COMBINE])
        combine_t = sb("combine_t", [COMBINE, 128])
        spread = sb("spread", [128, RING, GROUP])
        spread_sh = sb("spread_sh", [128, GROUP])
        act = sb("act", [128, 2, GROUP])
        h_hi = sb("h_hi", [128, 2, GROUP], f32r)
        h_lo = sb("h_lo", [128, 2, GROUP], f32r)

        gate_ps = [ps(f"gate_ps{i}", [128, GROUP]) for i in range(2)]
        up_ps = [ps(f"up_ps{i}", [128, GROUP]) for i in range(2)]
        out_ps = ps("out_ps", [128, PAIRS, D])
        att_ps = ps("att_ps", [128, 2, 512])
        bank_x, bank_y = att_ps[:, 0, :], att_ps[:, 1, :]

        raw_loaded = [sem(f"raw_loaded{i}") for i in range(STAGING)]
        small_loaded = sem("small_loaded")
        x_loaded = [sem(f"x_loaded{i}") for i in range(2)]
        ctx_loaded = sem("ctx_loaded")
        const_made = sem("const_made")
        pool_step = sem("pool_step")
        tanh_made = sem("tanh_made")
        w_hi_made, w_lo_made = sem("w_hi_made"), sem("w_lo_made")
        wr_step = sem("wr_step")
        norm1_step, queries_normed = sem("norm1_step"), sem("queries_normed")
        rstd1_made, rstd2_made = sem("rstd1_made"), sem("rstd2_made")
        transposed = sem("transposed")
        q_copied, k_copied, k_expanded = sem("q_copied"), sem("k_copied"), sem("k_expanded")
        scored, masked, maxed, shifted, probs_made = (sem(n) for n in (
            "scored", "masked", "maxed", "shifted", "probs_made"))
        probs_turned, pt_x_copied, pt_y_copied = (sem(n) for n in (
            "probs_turned", "pt_x_copied", "pt_y_copied"))
        v_made, valued, inv_made, att_scaled, x2_made = (sem(n) for n in (
            "v_made", "valued", "inv_made", "att_scaled", "x2_made"))
        norm2_step, x2_normed, x2_turned, x2t_hi_made, x2t_lo_made = (sem(n) for n in (
            "norm2_step", "x2_normed", "x2_turned", "x2t_hi_made", "x2t_lo_made"))
        routed, logits_copied, route_step, exps_made, combined = (sem(n) for n in (
            "routed", "logits_copied", "route_step", "exps_made", "combined"))
        combine_turned, combine_t_copied, combine_stored = (sem(n) for n in (
            "combine_turned", "combine_t_copied", "combine_stored"))
        spread_loaded = [sem(f"spread_loaded{i}") for i in range(RING)]
        spread_sh_loaded = sem("spread_sh_loaded")
        gate_ready, up_ready, tanh_ready, gated, upped, weighted, hi_ready, lo_ready, down_done = (
            sem(n) for n in ("gate_ready", "up_ready", "tanh_ready", "gated", "upped", "weighted",
                             "hi_ready", "lo_ready", "down_done"))
        y_ready, y_stored = sem("y_ready"), sem("y_stored")
        CONSTS = 7
        APART = (const_made, CONSTS)

        def run(eng, prepare, body, drain):
            prepare()
            body(None, None, 0)
            body(0, 0, 1)
            with eng.Fori(0, (groups - 2) // 2) as n:
                body(2 * n + 1, 1, 2 * n + 2)
                body(2 * n + 2, 0, 2 * n + 3)
            body(groups - 1, 1, None)
            drain()

        block = ctx.enter_context(nc.Block())

        @block.sync
        def _(sp):
            def load_x(pair, slot):
                row, used = known(sp, pair * PAIR), known(sp, pair - 1)
                after(sp, x2_made, used)
                sp.dma_start(x_in[:, slot, :], x_rows[bass.ds(row, PAIR), :])\
                    .then_inc(x_loaded[slot], 16)

            def load_ctx(pair):
                pair = known(sp, pair)
                batch = [known(sp, pair * 2 + b) for b in range(2)]
                after(sp, transposed, pair)
                after(sp, v_made, pair)
                for b in range(2):
                    src = ctx_in[bass.ds(batch[b], 1), :, :]\
                        .rearrange("b k (c n) -> (b k) c n", c=QUARTERS)
                    for copy in range(2):
                        rows = slice(copy * SEQ, (copy + 1) * SEQ)
                        sp.dma_start(ctx_k[rows, :, b, :], src).then_inc(ctx_loaded, 16)

            def load_weights(i):
                slot = i % STAGING
                after(sp, w_lo_made, i - STAGING + 1)
                after(sp, w_hi_made, i - STAGING + 1)
                gu = raw[:, slot, 0:2 * D].rearrange("p (k s f) -> p k s f", k=KC, s=2)
                if i < EXPERTS:
                    gate, up, down = w_gate[i, :, :], w_up[i, :, :], w_down[i, :, :]
                    n = 128
                else:
                    f0 = (i - EXPERTS) * 128
                    n = min(128, SHARED - f0)
                    gate, up = w_sh_gate[:, f0:f0 + n], w_sh_up[:, f0:f0 + n]
                    down = w_sh_down[f0:f0 + n, :]
                sp.dma_start(gu[:, :, 0, 0:n], gate.rearrange("(k p) f -> p k f", p=128))\
                    .then_inc(raw_loaded[slot], 16)
                sp.dma_start(gu[:, :, 1, 0:n], up.rearrange("(k p) f -> p k f", p=128))\
                    .then_inc(raw_loaded[slot], 16)
                sp.dma_start(raw[0:n, slot, 2 * D:3 * D], down).then_inc(raw_loaded[slot], 16)

            def store_combine(group, par, p):
                after(sp, combine_t_copied, known(sp, PAIRS * group + p + 1))
                sp.dma_start(combine_dram[par, :, p * PAIR:(p + 1) * PAIR], combine_t[:, :])\
                    .then_inc(combine_stored, 16)

            def load_spread(e, par, used):
                slot = spread[:, e % RING, :] if e < EXPERTS else spread_sh[:, :]
                loaded = spread_loaded[e % RING] if e < EXPERTS else spread_sh_loaded
                after(sp, weighted, used)
                sp.dma_start(slot, combine_dram[par, e:e + 1, :].broadcast_to([128, GROUP]))\
                    .then_inc(loaded, 16)

            def store_y(group, par):
                for p in range(PAIRS):
                    row, count = known(sp, group * GROUP + p * PAIR), known(sp, PAIRS * group + p + 1)
                    after(sp, y_ready, count)
                    sp.dma_start(out_rows[bass.ds(row, PAIR), :],
                                 x2[:, par, p, :]).then_inc(y_stored, 16)

            def prepare():
                sp.dma_start(x_in[:, 0, :], x_rows[0:PAIR, :]).then_inc(x_loaded[0], 16)
                load_ctx(0)
                for r in range(KC):
                    rows = slice(r * 128, r * 128 + 128)
                    sp.dma_start(wr_raw[:, r, 0:EXPERTS], w_router[rows, :]).then_inc(small_loaded, 16)
                    sp.dma_start(wr_raw[:, r, EXPERTS:COMBINE], w_sh_expert_gate[rows, :])\
                        .then_inc(small_loaded, 16)
                sp.dma_start(gates[:, 0:1], g_xattn.rearrange("(a n) -> a n", a=1).broadcast_to([128, 1]))\
                    .then_inc(small_loaded, 16)
                sp.dma_start(gates[:, 1:2], g_ffn.rearrange("(a n) -> a n", a=1).broadcast_to([128, 1]))\
                    .then_inc(small_loaded, 16)

            def body(ffn, par, att):
                for k in range(POINTS):
                    if att is not None:
                        a_par = 0 if ffn is None else 1 - par
                        for name, p in STAGES[k]:
                            if name == "load" and (ffn is not None or p > 0):
                                load_x(PAIRS * att + p, p % 2)
                                load_ctx(PAIRS * att + p)
                            if name == "weigh":
                                store_combine(att, a_par, p)
                    if ffn is None and k % 2 == 0:
                        load_weights(k // 2)
                    if ffn is not None and k % 2 == 1 and RING <= (k + 5) // 2 < EXPERTS:
                        e = (k + 5) // 2
                        load_spread(e, par, known(sp, CHUNKS * ffn + e - RING + 1))
                    if ffn is not None and k == 5 and not (isinstance(ffn, int) and ffn == 0):
                        store_y(ffn - 1, 1 - par)
                if att is not None:
                    a_par = 0 if ffn is None else 1 - par
                    stored = known(sp, 16 * PAIRS * (att + 1))
                    free = [known(sp, CHUNKS * (att - 1) + EXPERTS + e - RING + 1) for e in range(RING)]
                    after(sp, combine_stored, stored)
                    for e in range(RING):
                        load_spread(e, a_par, free[e])
                    load_spread(EXPERTS, a_par, known(sp, CHUNKS * att))

            def drain():
                store_y(groups - 1, (groups - 1) % 2)
                sp.wait_ge(y_stored, 16 * PAIRS * groups)
                sp.wait_ge(combine_stored, 16 * PAIRS * groups)

            run(sp, prepare, body, drain)

        @block.gpsimd
        def _(pool):
            steps = [0]

            def chain(ins):
                steps[0] += 1
                ins.then_inc(pool_step, 1)
                pool.wait_ge(pool_step, steps[0])

            def prepare():
                nc.gpsimd.memset(x_norm[:, :, :, :], 0.0).then_inc(const_made, 1)
                chain(nc.gpsimd.memset(minus_half[:, :], -0.5))
                chain(nc.gpsimd.memset(ident[:, :], 0.0))
                nc.gpsimd.affine_select(out=ident[:, :], in_=ident[:, :], compare_op=ALU.not_equal,
                                        fill=1.0, base=0, pattern=[[-1, 128]],
                                        channel_multiplier=1).then_inc(const_made, 1)
                chain(nc.gpsimd.memset(head_two[:, :, :], 1.0))
                chain(nc.gpsimd.affine_select(out=head_two[:, :, :], in_=head_two[:, :, :],
                                              compare_op=ALU.is_ge, fill=0.0, base=0,
                                              pattern=[[-SEQ, 2], [-HD, QUARTERS]],
                                              channel_multiplier=1))
                chain(nc.gpsimd.affine_select(out=head_two[:, :, :], in_=head_two[:, :, :],
                                              compare_op=ALU.is_ge, fill=0.0, base=HD - 1,
                                              pattern=[[SEQ, 2], [HD, QUARTERS]],
                                              channel_multiplier=-1))
                chain(nc.gpsimd.tensor_tensor(head_mask[:, :], head_two[:, 0, :], head_two[:, 1, :],
                                              ALU.add))
                chain(nc.gpsimd.memset(causal_f[:, :], 1.0))
                for b in range(2):
                    half = causal_f[b * SEQ:(b + 1) * SEQ, :]
                    last = nc.gpsimd.affine_select(out=half, in_=half, compare_op=ALU.is_ge, fill=0.0,
                                                   base=0, pattern=[[-1, SEQ]],
                                                   channel_multiplier=1)
                    chain(last)
                nc.gpsimd.tensor_copy(causal[:, :], causal_f[:, :]).then_inc(const_made, 1)
                nc.gpsimd.memset(scores[:, :, :], MASKED * HD ** 0.5).then_inc(const_made, 1)
                chain(nc.gpsimd.memset(v_block[:, :, :], 0.0))
                chain(nc.gpsimd.memset(v_block[0:SEQ, :, 4 * HD:4 * HD + 1], 1.0))
                chain(nc.gpsimd.memset(v_block[SEQ:128, :, 4 * HD + 1:4 * HD + 2], 1.0))
                nc.gpsimd.memset(logits[:, EXPERTS:], FAR)
                nc.gpsimd.memset(top_k[:, TOP_K:], FAR).then_inc(const_made, 1)
                nc.gpsimd.memset(wr_raw[:, :, COMBINE:ROUTES], 0.0).then_inc(const_made, 1)
                for w in (wgu_hi, wgu_lo):
                    chain(nc.gpsimd.memset(w[:, CHUNKS - 1, :, :, SHARED_REST:128].bitcast(f32), 0.0))
                for w in (wd_hi, wd_lo):
                    chain(nc.gpsimd.memset(w[SHARED_REST:128, CHUNKS - 1, :].bitcast(f32), 0.0))
                nc.gpsimd.memset(head_two[:, :, :], 0.0).then_inc(const_made, 1)

            def attention(name, p, group):
                pair = PAIRS * group + p
                if name in ("norm", "value"):
                    step, made, spread_ = ((norm1_step, rstd1_made, rstd) if name == "norm" else
                                           (norm2_step, rstd2_made, rstd2))
                    after(pool, step, 3 * (pair + 1))
                    nc.gpsimd.tensor_tensor(spread_[:, :], spread_[:, :], minus_half[:, :], ALU.pow)\
                        .then_inc(made, 1)
                if name == "transpose":
                    after(pool, k_copied, pair + 1)
                    nc.gpsimd.tensor_tensor(
                        k_block[:, :, :, :],
                        k_t[:, :, :].unsqueeze(2).broadcast_to([128, QUARTERS, QUARTERS, SEQ]),
                        head_mask[:, :].unsqueeze(1).unsqueeze(3)
                        .broadcast_to([128, QUARTERS, QUARTERS, SEQ]),
                        ALU.mult).then_inc(k_expanded, 1)
                    loaded, used = known(pool, 64 * (pair + 1)), known(pool, pair)
                    expanded = known(pool, pair + 1)
                    after(pool, *APART)
                    after(pool, ctx_loaded, loaded)
                    after(pool, valued, used)
                    after(pool, k_expanded, expanded)
                    for h in range(2):
                        rows = slice(h * SEQ, (h + 1) * SEQ)
                        dst = v_block[rows, :, 0:4 * HD].rearrange("p j (b h d) -> p j b h d", b=2, h=2)
                        src = ctx_k[rows, :, :, :].rearrange("p c b (j h d) -> p c j b h d", h=2, d=HD)
                        for j in range(2):
                            last = nc.gpsimd.tensor_copy(dst[:, j::2, :, h, :], src[:, :, j, :, h, :])
                    last.then_inc(v_made, 1)
                    after(pool, v_made, pair + 1)
                if name == "score":
                    after(pool, maxed, pair + 1)
                    nc.gpsimd.tensor_tensor(probs[:, :, :], scores[:, :, :],
                                            row_max[:, :].unsqueeze(2).broadcast_to([128, HEADS, SEQ]),
                                            ALU.subtract).then_inc(shifted, 1)

            def weigh_hidden(group, i):
                n = CHUNKS * group + i
                if i < EXPERTS:
                    after(pool, spread_loaded[i % RING], 16 * ((EXPERTS // RING) * group + i // RING + 1))
                    row = spread[:, i % RING, :]
                else:
                    after(pool, spread_sh_loaded, 16 * (group + 1))
                    row = spread_sh[:, :]
                after(pool, upped, n + 1)
                nc.gpsimd.tensor_tensor(act[:, i % 2, :], act[:, i % 2, :], row, ALU.mult)\
                    .then_inc(weighted, 1)

            def body(ffn, par, att):
                for k in range(POINTS):
                    if ffn is not None and k % 2 == 1:
                        weigh_hidden(ffn, k // 2)
                    if att is not None:
                        for name, p in STAGES[k]:
                            attention(name, p, att)

            run(pool, prepare, body, lambda: None)

        @block.scalar
        def _(sc):
            def prepare():
                sc.wait_ge(small_loaded, 16 * (2 * KC + 2))
                nc.scalar.activation(gate_tanh[:, :], gates[:, :], ACT.Tanh).then_inc(tanh_made, 1)

            def attention(name, p, group, par):
                pair = PAIRS * group + p
                if name == "transpose":
                    sc.wait_ge(transposed, pair + 1)
                    nc.scalar.activation(q_t[:, :, :], bank_x.rearrange("p (c t) -> p c t", t=128),
                                         ACT.Copy).then_inc(q_copied, 1)
                if name == "score":
                    sc.wait_ge(shifted, pair + 1)
                    nc.scalar.activation(probs[:, :, :], probs[:, :, :], ACT.Exp, scale=HD ** -0.5)\
                        .then_inc(probs_made, 1)
                if name == "turn":
                    sc.wait_ge(probs_turned, pair + 1)
                    nc.scalar.activation(p_t[:, 0:4, :], bank_x.rearrange("p (j t) -> p j t", t=128),
                                         ACT.Copy).then_inc(pt_x_copied, 1)
                if name == "project":
                    sc.wait_ge(x2_turned, pair + 1)
                    nc.scalar.activation(x2t_hi[:, par, :, p * PAIR:(p + 1) * PAIR],
                                         bank_x[:, 0:D].rearrange("p (c t) -> p c t", t=128),
                                         ACT.Copy).then_inc(x2t_hi_made, 1)
                if name == "route":
                    sc.wait_ge(route_step, 4 * pair + 4)
                    nc.scalar.activation(exped[:, :], exponent[:, :], ACT.Exp).then_inc(exps_made, 1)

            def weights_hi(i):
                slot = i % STAGING
                sc.wait_ge(raw_loaded[slot], 48 * (i // STAGING + 1))
                n = 128 if i < CHUNKS - 1 else SHARED_REST
                gu = raw[:, slot, 0:2 * D].rearrange("p (k s f) -> p k s f", k=KC, s=2)
                if n < 128:
                    sc.wait_ge(const_made, CONSTS)
                nc.scalar.activation(wgu_hi[:, i, :, :, 0:n], gu[:, :, :, 0:n], ACT.Copy)
                nc.scalar.activation(wd_hi[0:n, i, :], raw[0:n, slot, 2 * D:3 * D], ACT.Copy)\
                    .then_inc(w_hi_made, 1)

            def body(ffn, par, att):
                for k in range(POINTS):
                    if att is not None:
                        for name, p in STAGES[k]:
                            attention(name, p, att, 0 if ffn is None else 1 - par)
                    i = k // 2
                    if ffn is None and k % 2 == 0:
                        weights_hi(i)
                    if ffn is not None and k % 2 == 0:
                        n = CHUNKS * ffn + i
                        after(sc, lo_ready, n - 1)
                        after(sc, gate_ready, n + 1)
                        nc.scalar.activation(act[:, i % 2, :], gate_ps[i % 2][:, :], ACT.Tanh, scale=0.5)\
                            .then_inc(tanh_ready, 1)
                    if ffn is not None and k % 2 == 1:
                        n = CHUNKS * ffn + i
                        after(sc, weighted, n + 1)
                        after(sc, down_done, n - 1)
                        nc.scalar.activation(h_hi[:, i % 2, :], act[:, i % 2, :], ACT.Copy)\
                            .then_inc(hi_ready, 1)

            run(sc, prepare, body, lambda: None)

        @block.vector
        def _(ve):
            def prepare():
                ve.wait_ge(small_loaded, 16 * (2 * KC + 2))
                ve.wait_ge(const_made, CONSTS)
                nc.vector.tensor_copy(wr_hi[:, :, :], wr_raw[:, :, :]).then_inc(wr_step, 1)
                ve.wait_ge(wr_step, 1)
                nc.vector.tensor_tensor(wr_lo[:, :, :], wr_raw[:, :, :], wr_hi[:, :, :].bitcast(f32),
                                        ALU.subtract).then_inc(wr_step, 1)

            def attention(name, p, group, par):
                pair = PAIRS * group + p
                if name == "norm":
                    src = x_in[:, p % 2, :]
                    after(ve, x_loaded[p % 2], 16 * (2 * group + p // 2 + 1))
                    nc.vector.bn_stats(stats[:, :], src).then_inc(norm1_step, 1)
                    after(ve, norm1_step, 3 * pair + 1, APART)
                    nc.vector.bn_aggr(moments[:, :], stats[:, :]).then_inc(norm1_step, 1)
                    after(ve, norm1_step, 3 * pair + 2)
                    nc.vector.tensor_scalar(rstd[:, :], moments[:, 1:2], EPS, None, ALU.add)\
                        .then_inc(norm1_step, 1)
                    after(ve, rstd1_made, pair + 1)
                    after(ve, transposed, pair)
                    for b in range(2):
                        rows = slice(b * SEQ, (b + 1) * SEQ)
                        last = nc.vector.tensor_scalar(
                            x_norm[rows, :, b, :], src[rows, :].rearrange("p (c n) -> p c n", c=QUARTERS),
                            moments[rows, 0:1], rstd[rows, :], ALU.subtract, ALU.mult)
                    last.then_inc(queries_normed, 1)
                if name == "transpose":
                    after(ve, transposed, pair + 1)
                    nc.vector.tensor_copy(k_t[:, :, :],
                                          bank_y[:, 0:QUARTERS * SEQ].rearrange("p (c k) -> p c k", k=SEQ))\
                        .then_inc(k_copied, 1)
                if name == "score":
                    after(ve, scored, pair + 1, APART)
                    mask = causal[:, :].unsqueeze(1).broadcast_to([128, HEADS // 2, SEQ])
                    for c in range(2):
                        last = nc.vector.copy_predicated(
                            scores[:, c * 8:(c + 1) * 8, :], mask,
                            att_ps[:, c, :].rearrange("p (h k) -> p h k", k=SEQ))
                    last.then_inc(masked, 1)
                    after(ve, masked, pair + 1)
                    nc.vector.tensor_reduce(row_max[:, :], scores[:, :, :], AX.X, ALU.max)\
                        .then_inc(maxed, 1)
                if name == "turn":
                    after(ve, probs_turned, pair + 1)
                    nc.vector.tensor_copy(p_t[:, 4:8, :], bank_y.rearrange("p (j t) -> p j t", t=128))\
                        .then_inc(pt_y_copied, 1)
                if name == "value":
                    after(ve, valued, pair + 1)
                    pv = att_ps[:, :, 0:4 * VCOLS].rearrange("p c (j v) -> p c j v", v=VCOLS)
                    nc.vector.reciprocal(
                        inv_sum[:, :].rearrange("p (c j h) -> p c j h", c=2, j=4),
                        pv[:, :, :, 4 * HD:VCOLS]).then_inc(inv_made, 1)
                    after(ve, inv_made, pair + 1)
                    for b in range(2):
                        rows = slice(b * SEQ, (b + 1) * SEQ)
                        for c in range(2):
                            last = nc.vector.tensor_tensor(
                                attended[rows, c * 128:(c + 1) * 128]
                                .rearrange("p (j h d) -> p j h d", j=4, h=2),
                                pv[rows, c, :, 2 * HD * b:2 * HD * (b + 1)]
                                .rearrange("p j (h d) -> p j h d", h=2),
                                inv_sum[rows, c * 8:(c + 1) * 8].rearrange("p (j h) -> p j h", h=2)
                                .unsqueeze(3).broadcast_to([SEQ, 4, 2, HD]),
                                ALU.mult)
                    last.then_inc(att_scaled, 1)
                    after(ve, att_scaled, pair + 1)
                    if isinstance(group, int) and group == 0:
                        ve.wait_ge(tanh_made, 1)
                    if p == 0:
                        after(ve, y_stored, 16 * PAIRS * (group - 1))
                    nc.vector.scalar_tensor_tensor(
                        out=x2[:, par, p, :], in0=attended[:, :], scalar=gate_tanh[:, 0:1],
                        in1=x_in[:, p % 2, :], op0=ALU.mult, op1=ALU.add).then_inc(x2_made, 1)
                    after(ve, x2_made, pair + 1)
                    src = x2[:, par, p, :]
                    nc.vector.bn_stats(stats2[:, :], src).then_inc(norm2_step, 1)
                    after(ve, norm2_step, 3 * pair + 1, APART)
                    nc.vector.bn_aggr(moments2[:, :], stats2[:, :]).then_inc(norm2_step, 1)
                    after(ve, norm2_step, 3 * pair + 2)
                    nc.vector.tensor_scalar(rstd2[:, :], moments2[:, 1:2], EPS, None, ALU.add)\
                        .then_inc(norm2_step, 1)
                    after(ve, rstd2_made, pair + 1)
                    nc.vector.tensor_scalar(x2_norm[:, :], src, moments2[:, 0:1], rstd2[:, :],
                                            ALU.subtract, ALU.mult).then_inc(x2_normed, 1)
                if name == "project":
                    after(ve, x2t_hi_made, pair + 1)
                    where = slice(p * PAIR, (p + 1) * PAIR)
                    nc.vector.tensor_tensor(x2t_lo[:, par, :, where],
                                            bank_x[:, 0:D].rearrange("p (c t) -> p c t", t=128),
                                            x2t_hi[:, par, :, where].bitcast(f32), ALU.subtract)\
                        .then_inc(x2t_lo_made, 1)
                if name == "route":
                    after(ve, routed, pair + 1)
                    nc.vector.tensor_copy(logits[:, 0:EXPERTS], bank_y[:, 0:EXPERTS])
                    nc.vector.tensor_scalar(exponent[:, EXPERTS:COMBINE], bank_y[:, EXPERTS:COMBINE],
                                            -1.0, None, ALU.mult).then_inc(logits_copied, 1)
                    after(ve, logits_copied, pair + 1, APART)
                    nc.vector.max(top8[:, :], logits[:, 0:EXPERTS]).then_inc(route_step, 1)
                    after(ve, route_step, 4 * pair + 1)
                    nc.vector.tensor_copy(top_k[:, 0:TOP_K], top8[:, 0:TOP_K]).then_inc(route_step, 1)
                    after(ve, route_step, 4 * pair + 2, APART)
                    nc.vector.match_replace(replaced[:, :], top_k[:, :], logits[:, :], -FAR)\
                        .then_inc(route_step, 1)
                    nc.vector.tensor_scalar(exponent[:, 0:EXPERTS], logits[:, 0:EXPERTS], top8[:, 0:1],
                                            None, ALU.subtract).then_inc(route_step, 1)
                    after(ve, route_step, 4 * pair + 4)
                    nc.vector.tensor_tensor(chosen[:, :], replaced[:, 0:EXPERTS], logits[:, 0:EXPERTS],
                                            ALU.not_equal).then_inc(combined, 1)
                    after(ve, combined, 6 * pair + 1)
                    after(ve, exps_made, pair + 1)
                    nc.vector.scalar_tensor_tensor(
                        out=weighed[:, :], in0=exped[:, 0:EXPERTS], scalar=1.0, in1=chosen[:, :],
                        op0=ALU.mult, op1=ALU.mult, accum_out=sums[:, 0:1]).then_inc(combined, 1)
                    nc.vector.tensor_scalar(sums[:, 1:2], exped[:, EXPERTS:COMBINE], 1.0, None, ALU.add)\
                        .then_inc(combined, 1)
                    after(ve, combined, 6 * pair + 3)
                    nc.vector.reciprocal(inv_sums[:, :], sums[:, :]).then_inc(combined, 1)
                    after(ve, combined, 6 * pair + 4)
                    nc.vector.tensor_scalar(combine[:, 0:EXPERTS], weighed[:, :], inv_sums[:, 0:1], 0.5,
                                            ALU.mult, ALU.mult).then_inc(combined, 1)
                    nc.vector.tensor_scalar(combine[:, EXPERTS:COMBINE], inv_sums[:, 1:2], 0.5, None,
                                            ALU.mult).then_inc(combined, 1)
                if name == "weigh":
                    after(ve, combine_turned, pair + 1)
                    after(ve, combine_stored, 16 * pair)
                    nc.vector.tensor_copy(combine_t[:, :], bank_y[0:COMBINE, 0:128])\
                        .then_inc(combine_t_copied, 1)

            def weights_lo(i):
                slot = i % STAGING
                ve.wait_ge(w_hi_made, i + 1)
                n = 128 if i < CHUNKS - 1 else SHARED_REST
                gu = raw[:, slot, 0:2 * D].rearrange("p (k s f) -> p k s f", k=KC, s=2)
                nc.vector.tensor_tensor(wgu_lo[:, i, :, :, 0:n], gu[:, :, :, 0:n],
                                        wgu_hi[:, i, :, :, 0:n].bitcast(f32), ALU.subtract)
                nc.vector.tensor_tensor(wd_lo[0:n, i, :], raw[0:n, slot, 2 * D:3 * D],
                                        wd_hi[0:n, i, :].bitcast(f32), ALU.subtract)\
                    .then_inc(w_lo_made, 1)

            def split_lo(n, slot):
                after(ve, hi_ready, n + 1)
                nc.vector.tensor_tensor(h_lo[:, slot, :], act[:, slot, :], h_hi[:, slot, :].bitcast(f32),
                                        ALU.subtract).then_inc(lo_ready, 1)

            def finish_group(group, par):
                after(ve, down_done, CHUNKS * (group + 1))
                for p in range(PAIRS):
                    nc.vector.scalar_tensor_tensor(
                        out=x2[:, par, p, :], in0=out_ps[:, p, :], scalar=gate_tanh[:, 1:2],
                        in1=x2[:, par, p, :], op0=ALU.mult, op1=ALU.add).then_inc(y_ready, 1)

            def body(ffn, par, att):
                first = isinstance(ffn, int) and ffn == 0
                for k in range(POINTS):
                    if att is not None:
                        for name, p in STAGES[k]:
                            attention(name, p, att, 0 if ffn is None else 1 - par)
                    i = k // 2
                    if ffn is None and k % 2 == 0:
                        weights_lo(i)
                    if ffn is not None and k % 2 == 0:
                        n = CHUNKS * ffn + i
                        if not (first and i == 0):
                            split_lo(n - 1, (i - 1) % 2)
                        a = act[:, i % 2, :]
                        after(ve, tanh_ready, n + 1)
                        nc.vector.scalar_tensor_tensor(out=a, in0=a, scalar=1.0, in1=gate_ps[i % 2][:, :],
                                                       op0=ALU.add, op1=ALU.mult).then_inc(gated, 1)
                        after(ve, up_ready, n + 1)
                        after(ve, gated, n + 1)
                        nc.vector.tensor_tensor(a, a, up_ps[i % 2][:, :], ALU.mult).then_inc(upped, 1)
                    if k == 4 and ffn is not None and not first:
                        finish_group(ffn - 1, 1 - par)

            def drain():
                split_lo(CHUNKS * groups - 1, (CHUNKS - 1) % 2)
                finish_group(groups - 1, (groups - 1) % 2)

            run(ve, prepare, body, drain)

        @block.tensor
        def _(te):
            def three(out_ap, a_hi, a_lo, b_hi, b_lo, first, last, check=False):
                nc.tensor.matmul(out_ap, a_hi, b_hi, start=first, stop=False, skip_group_check=check)
                nc.tensor.matmul(out_ap, a_hi, b_lo, start=False, stop=False, skip_group_check=check)
                return nc.tensor.matmul(out_ap, a_lo, b_hi, start=False, stop=last,
                                        skip_group_check=check)

            def attention(name, p, group, par):
                pair = PAIRS * group + p
                if name == "transpose":
                    after(te, queries_normed, pair + 1)
                    after(te, ctx_loaded, 64 * (pair + 1))
                    after(te, x2t_lo_made, pair)
                    after(te, combine_t_copied, pair - 1 if p else pair)
                    for c in range(QUARTERS):
                        nc.tensor.transpose(bank_x[:, c * 128:(c + 1) * 128],
                                            x_norm[:, c, :, :].rearrange("p b n -> p (b n)"), ident[:, :])
                    for c in range(QUARTERS):
                        last = nc.tensor.transpose(bank_y[:, c * SEQ:(c + 1) * SEQ],
                                                   ctx_k[0:SEQ, c, :, :].rearrange("p b n -> p (b n)"),
                                                   ident[0:SEQ, 0:SEQ])
                    last.then_inc(transposed, 1)
                if name == "score":
                    after(te, q_copied, pair + 1)
                    after(te, k_expanded, pair + 1)
                    after(te, logits_copied, pair if p else 0)
                    for c in range(QUARTERS):
                        last = nc.tensor.matmul(
                            att_ps[:, c // 2, (c % 2) * 256:(c % 2 + 1) * 256], q_t[:, c, :],
                            k_block[:, c, :, :].rearrange("p h k -> p (h k)"), start=True, stop=True)
                    last.then_inc(scored, 1)
                if name == "turn":
                    after(te, probs_made, pair + 1)
                    after(te, combine_t_copied, pair if p else 0)
                    for j in range(HEADS // 2):
                        last = nc.tensor.transpose(
                            att_ps[:, j // 4, (j % 4) * 128:(j % 4 + 1) * 128],
                            probs[:, 2 * j:2 * j + 2, :].rearrange("p h k -> p (h k)"), ident[:, :])
                    last.then_inc(probs_turned, 1)
                if name == "value":
                    after(te, pt_x_copied, pair + 1)
                    after(te, pt_y_copied, pair + 1)
                    after(te, v_made, pair + 1)
                    for j in range(HEADS // 2):
                        last = nc.tensor.matmul(
                            att_ps[:, j // 4, (j % 4) * VCOLS:(j % 4 + 1) * VCOLS], p_t[:, j, :],
                            v_block[:, j, :], start=True, stop=True)
                    last.then_inc(valued, 1)
                if name == "project":
                    after(te, x2_normed, pair + 1)
                    for c in range(KC):
                        last = nc.tensor.transpose(bank_x[:, c * 128:(c + 1) * 128],
                                                   x2_norm[:, c * 128:(c + 1) * 128], ident[:, :])
                    last.then_inc(x2_turned, 1)
                if name == "route":
                    after(te, x2t_lo_made, pair + 1)
                    if p < PAIRS - 1:
                        after(te, k_copied, pair + 2)
                    where = slice(p * PAIR, (p + 1) * PAIR)
                    for c in range(KC):
                        last = three(bank_y[:, 0:ROUTES], x2t_hi[:, par, c, where],
                                     x2t_lo[:, par, c, where], wr_hi[:, c, :], wr_lo[:, c, :],
                                     c == 0, c == KC - 1)
                    last.then_inc(routed, 1)
                if name == "weigh":
                    after(te, combined, 6 * (pair + 1))
                    if p < PAIRS - 1:
                        after(te, masked, pair + 2)
                    nc.tensor.transpose(bank_y[0:COMBINE, 0:128], combine[:, :], ident[:, :])\
                        .then_inc(combine_turned, 1)

            def gate_up(group, par, i):
                n = CHUNKS * group + i
                after(te, gated, n - 1)
                if isinstance(group, int) and group == 0:
                    te.wait_ge(w_lo_made, i + 1)
                for s, bank, ready in ((0, gate_ps, gate_ready), (1, up_ps, up_ready)):
                    if s:
                        after(te, upped, n - 1)
                    for c in range(KC):
                        last = three(bank[i % 2][:, :], wgu_hi[:, i, c, s, :], wgu_lo[:, i, c, s, :],
                                     x2t_hi[:, par, c, :], x2t_lo[:, par, c, :], c == 0, c == KC - 1)
                    last.then_inc(ready, 1)

            def down(group, i):
                n = CHUNKS * group + i
                after(te, lo_ready, n + 1)
                if i == 0:
                    after(te, y_ready, PAIRS * group)
                for p in range(PAIRS):
                    where = slice(p * PAIR, (p + 1) * PAIR)
                    last = three(out_ps[:, p, :], h_hi[:, i % 2, where], h_lo[:, i % 2, where],
                                 wd_hi[:, i, :], wd_lo[:, i, :], i == 0 and p % 2 == 0,
                                 i == CHUNKS - 1, True)
                last.then_inc(down_done, 1)

            def prepare():
                te.wait_ge(const_made, CONSTS)
                te.wait_ge(wr_step, 2)

            def body(ffn, par, att):
                first = isinstance(ffn, int) and ffn == 0
                for k in range(POINTS):
                    if att is not None:
                        for name, p in STAGES[k]:
                            attention(name, p, att, 0 if ffn is None else 1 - par)
                    i = k // 2
                    if ffn is not None and k % 2 == 0:
                        gate_up(ffn, par, i)
                    if ffn is not None and k % 2 == 1:
                        if i >= 2:
                            down(ffn, i - 2)
                        elif not first:
                            down(ffn - 1, CHUNKS + i - 2)

            def drain():
                down(groups - 1, CHUNKS - 2)
                down(groups - 1, CHUNKS - 1)

            run(te, prepare, body, drain)


_INS = ["x", "ctx_2048", "g_xattn", "g_ffn", "L0_ffn_w_router", "L0_ffn_w_gate", "L0_ffn_w_up",
        "L0_ffn_w_down", "L0_ffn_w_sh_gate", "L0_ffn_w_sh_up", "L0_ffn_w_sh_down",
        "L0_ffn_w_sh_expert_gate"]


def kernel(**inputs):
    import numpy as _np
    import concourse.bacc as _bacc
    from concourse import mybir as _mybir
    from concourse.bass_utils import run_bass_kernel_spmd as _run

    nc = _bacc.Bacc("TRN2", target_bir_lowering=False, num_devices=1, dynamic_dma_scratch_size=1024)
    arrays, args = {}, []
    for name in _INS:
        a = _np.ascontiguousarray(inputs[name])
        arrays[f"in_{name}"] = a
        args.append(nc.dram_tensor(f"in_{name}", a.shape, _mybir.dt.from_np(a.dtype),
                                   kind="ExternalInput").ap())
    shape = inputs["x"].shape
    args.append(nc.dram_tensor("out_0", shape, _mybir.dt.float32, kind="ExternalOutput").ap())
    flamingo_block(nc, *args)
    r = _run(nc, [arrays], core_ids=[0])
    return r.results[0]["out_0"]
```

```python
import concourse.bass as bass
from concourse import mybir
from contextlib import ExitStack

D = 256
KC = D // 128
SEQ = 64
HEADS, HD = 16, 16
EXPERTS, TOP_K = 16, 4
SHARED = 704
SHARED_CHUNKS = -(-SHARED // 128)
SHARED_REST = SHARED - 128 * (SHARED_CHUNKS - 1)
CHUNKS = EXPERTS + SHARED_CHUNKS
PAIR = 2 * SEQ
PAIRS = 4
GROUP = PAIRS * PAIR
QUARTERS = 4
POINTS = 2 * CHUNKS
ROUTES = EXPERTS + 2
COMBINE = EXPERTS + 1
RING = 4
STAGING = 4
VCOLS = 2 * 2 * HD + 2
MASKED = -10000.0
EPS = 1e-5
FAR = 3.0e38

FIRST_POINT, PERIOD = 1, 9
STEPS = {
    "PE": {"transpose": (0, 0), "score": (2, 2), "turn": (5, 5), "value": (6, 6),
           "project": (10, 8), "route": (12, 10), "weigh": (16, 12)},
    "SP": {"load_x": (7, 7), "load_ctx": (1, 1), "weigh": (16, 12)},
    "Pool": {"norm": (-2, -2), "expand": (0, 0), "shift": (3, 3), "value": (6.5, 6.5)},
    "ACT": {"values": (-1.5, -1.5), "transpose": (0, 0), "score": (3.5, 3.5), "turn": (5, 5), "project": (10, 8),
            "route": (12.5, 10.5)},
    "DVE": {"norm": (-2, -2), "transpose": (0, 0), "score": (2, 2), "turn": (5, 5), "value": (6, 6),
            "project": (10, 8), "route": (12, 10), "combine": (13, 11), "weigh": (16, 12)},
}


def steps_by_point(engine):
    at = [([], []) for _ in range(POINTS)]
    for p in range(PAIRS):
        for name, offsets in STEPS[engine].items():
            when = max(0, FIRST_POINT + PERIOD * p + offsets[p == PAIRS - 1])
            at[int(when)][when != int(when)].append((when, p, name))
    return [[[(name, p) for _, p, name in sorted(part, key=lambda s: s[:2])] for part in parts]
            for parts in at]


def known(eng, value):
    return value if isinstance(value, int) else eng.snap(eng.to_reg(value))


def after(eng, sem, count, apart=None):
    if apart is not None and not isinstance(count, int):
        count = known(eng, count)
        eng.wait_ge(*apart)
    if not isinstance(count, int) or count > 0:
        eng.wait_ge(sem, count)


def flamingo_block(nc, x, ctx_in, g_xattn, g_ffn, w_router, w_gate, w_up, w_down, w_sh_gate, w_sh_up,
                   w_sh_down, w_sh_expert_gate, out):
    f32, f32r, u8 = mybir.dt.float32, mybir.dt.float32r, mybir.dt.uint8
    ALU, ACT, AX = mybir.AluOpType, mybir.ActivationFunctionType, mybir.AxisListType

    tokens = x.shape[0] * x.shape[1]
    groups = tokens // GROUP
    x_rows = x.rearrange("b s d -> (b s) d")
    out_rows = out.rearrange("b s d -> (b s) d")
    combine_dram = nc.dram_tensor("combine_rows", (2, COMBINE, GROUP), f32, kind="Internal").ap()

    ctx = ExitStack()
    with ctx:
        def sb(name, shape, dt=f32):
            return ctx.enter_context(nc.sbuf_tensor(name, shape, dt))

        def ps(name, shape):
            return ctx.enter_context(nc.psum_tensor(name, shape, f32))

        def sem(name):
            return ctx.enter_context(nc.semaphore(name))

        wgu_hi = sb("wgu_hi", [128, CHUNKS, 2 * D], f32r)
        wgu_lo = sb("wgu_lo", [128, CHUNKS, 2 * D], f32r)
        wd_hi = sb("wd_hi", [128, CHUNKS, D], f32r)
        wd_lo = sb("wd_lo", [128, CHUNKS, D], f32r)
        wr_hi = sb("wr_hi", [128, KC, ROUTES], f32r)
        wr_lo = sb("wr_lo", [128, KC, ROUTES], f32r)
        wr_raw = sb("wr_raw", [128, KC, ROUTES])
        raw = sb("raw", [128, STAGING, 3 * D])
        ident = sb("ident", [128, 128])
        head_mask = sb("head_mask", [128, QUARTERS])
        head_two = sb("head_two", [128, 2, QUARTERS])
        causal_f = sb("causal_f", [128, SEQ])
        causal = sb("causal", [128, SEQ], u8)
        minus_half = sb("minus_half", [128, 1])
        gates = sb("gates", [128, 2])
        gate_tanh = sb("gate_tanh", [128, 2])
        x_in = sb("x_in", [128, 2, D])
        ctx_k = sb("ctx_k", [128, QUARTERS, 2, SEQ])
        stats = sb("stats", [128, 6])
        moments = sb("moments", [128, 2])
        rstd = sb("rstd", [128, 1])
        stats2 = sb("stats2", [128, 6])
        moments2 = sb("moments2", [128, 2])
        rstd2 = sb("rstd2", [128, 1])
        x_norm = sb("x_norm", [128, QUARTERS, 2, SEQ])
        q_t = sb("q_t", [128, QUARTERS, 128])
        k_t = sb("k_t", [128, QUARTERS, SEQ])
        k_block = sb("k_block", [128, QUARTERS, QUARTERS, SEQ])
        p_t = k_block[:, :, :, :].rearrange("p a b c -> p (a b c)").rearrange("p (j t) -> p j t", t=128)
        scores = sb("scores", [128, HEADS, SEQ])
        row_max = sb("row_max", [128, HEADS])
        probs = sb("probs", [128, HEADS, SEQ])
        v_block = sb("v_block", [128, HEADS // 2, VCOLS])
        inv_sum = sb("inv_sum", [128, HEADS])
        attended = sb("attended", [128, D])
        x2 = sb("x2", [128, 2, PAIRS, D])
        x2_norm = sb("x2_norm", [128, D])
        x2t_hi = sb("x2t_hi", [128, 2, KC, GROUP], f32r)
        x2t_lo = sb("x2t_lo", [128, 2, KC, GROUP], f32r)
        logits = sb("logits", [128, EXPERTS + 8 - TOP_K])
        top8 = sb("top8", [128, 8])
        top_k = sb("top_k", [128, 8])
        replaced = sb("replaced", [128, EXPERTS + 8 - TOP_K])
        exponent = sb("exponent", [128, COMBINE])
        exped = sb("exped", [128, COMBINE])
        chosen = sb("chosen", [128, EXPERTS])
        weighed = sb("weighed", [128, EXPERTS])
        sums = sb("sums", [128, 2])
        inv_sums = sb("inv_sums", [128, 2])
        combine = sb("combine", [128, COMBINE])
        combine_t = sb("combine_t", [COMBINE, 128])
        spread = sb("spread", [128, RING, GROUP])
        spread_sh = sb("spread_sh", [128, GROUP])
        act = sb("act", [128, 2, GROUP])
        h_hi = sb("h_hi", [128, 2, GROUP], f32r)
        h_lo = sb("h_lo", [128, 2, GROUP], f32r)

        gate_ps = [ps(f"gate_ps{i}", [128, GROUP]) for i in range(2)]
        up_ps = [ps(f"up_ps{i}", [128, GROUP]) for i in range(2)]
        out_ps = ps("out_ps", [128, PAIRS, D])
        att_ps = ps("att_ps", [128, 2, 512])
        bank_x, bank_y = att_ps[:, 0, :], att_ps[:, 1, :]

        raw_loaded = [sem(f"raw_loaded{i}") for i in range(STAGING)]
        small_loaded = sem("small_loaded")
        x_loaded = [sem(f"x_loaded{i}") for i in range(2)]
        ctx_loaded = sem("ctx_loaded")
        const_made = sem("const_made")
        pool_step = sem("pool_step")
        tanh_made = sem("tanh_made")
        w_hi_made, w_lo_made = sem("w_hi_made"), sem("w_lo_made")
        wr_step = sem("wr_step")
        norm1_step, queries_normed = sem("norm1_step"), sem("queries_normed")
        rstd1_made, rstd2_made = sem("rstd1_made"), sem("rstd2_made")
        transposed = sem("transposed")
        q_copied, k_copied, k_expanded = sem("q_copied"), sem("k_copied"), sem("k_expanded")
        scored, masked, maxed, shifted, probs_made = (sem(n) for n in (
            "scored", "masked", "maxed", "shifted", "probs_made"))
        probs_turned, pt_x_copied, pt_y_copied = (sem(n) for n in (
            "probs_turned", "pt_x_copied", "pt_y_copied"))
        v_made, valued, inv_made, att_scaled, x2_made = (sem(n) for n in (
            "v_made", "valued", "inv_made", "att_scaled", "x2_made"))
        norm2_step, x2_normed, x2_turned, x2t_hi_made, x2t_lo_made = (sem(n) for n in (
            "norm2_step", "x2_normed", "x2_turned", "x2t_hi_made", "x2t_lo_made"))
        routed, logits_copied, route_step, exps_made, combined = (sem(n) for n in (
            "routed", "logits_copied", "route_step", "exps_made", "combined"))
        combine_turned, combine_t_copied, combine_stored = (sem(n) for n in (
            "combine_turned", "combine_t_copied", "combine_stored"))
        spread_loaded = [sem(f"spread_loaded{i}") for i in range(RING)]
        spread_sh_loaded = sem("spread_sh_loaded")
        gate_ready, up_ready, tanh_ready, gated, upped, weighted, hi_ready, lo_ready, down_done = (
            sem(n) for n in ("gate_ready", "up_ready", "tanh_ready", "gated", "upped", "weighted",
                             "hi_ready", "lo_ready", "down_done"))
        y_ready, y_stored = sem("y_ready"), sem("y_stored")
        CONSTS = 5
        APART = (const_made, CONSTS)

        def rows_of(i):
            return slice(0, 128 if i < CHUNKS - 1 else SHARED_REST)

        def gate_up_of(flat, i):
            n = 128 if i < CHUNKS - 1 else SHARED_REST
            return flat[:, 0:2 * KC * n].rearrange("p (k s f) -> p k s f", k=KC, s=2)

        def run(eng, prepare, body, drain):
            prepare()
            body(None, None, 0)
            body(0, 0, 1)
            with eng.Fori(0, (groups - 2) // 2) as n:
                body(2 * n + 1, 1, 2 * n + 2)
                body(2 * n + 2, 0, 2 * n + 3)
            body(groups - 1, 1, None)
            drain()

        block = ctx.enter_context(nc.Block())

        @block.sync
        def _(sp):
            def load_x(pair, before, slot):
                row, used = known(sp, pair * PAIR), known(sp, before)
                after(sp, x2_made, used)
                sp.dma_start(x_in[:, slot, :], x_rows[bass.ds(row, PAIR), :])\
                    .then_inc(x_loaded[slot], 16)

            def load_ctx(pair, before):
                before = known(sp, before)
                batch = [known(sp, pair * 2 + b) for b in range(2)]
                after(sp, transposed, before)
                after(sp, v_made, before)
                for b in range(2):
                    src = ctx_in[bass.ds(batch[b], 1), :, :]\
                        .rearrange("b k (c n) -> (b k) c n", c=QUARTERS)
                    for copy in range(2):
                        rows = slice(copy * SEQ, (copy + 1) * SEQ)
                        sp.dma_start(ctx_k[rows, :, b, :], src).then_inc(ctx_loaded, 16)

            def load_weights(i):
                slot = i % STAGING
                after(sp, w_lo_made, i - STAGING + 1)
                after(sp, w_hi_made, i - STAGING + 1)
                gu = gate_up_of(raw[:, slot, 0:2 * D], i)
                if i < EXPERTS:
                    gate, up, down = w_gate[i, :, :], w_up[i, :, :], w_down[i, :, :]
                    n = 128
                else:
                    f0 = (i - EXPERTS) * 128
                    n = min(128, SHARED - f0)
                    gate, up = w_sh_gate[:, f0:f0 + n], w_sh_up[:, f0:f0 + n]
                    down = w_sh_down[f0:f0 + n, :]
                sp.dma_start(gu[:, :, 0, :], gate.rearrange("(k p) f -> p k f", p=128))\
                    .then_inc(raw_loaded[slot], 16)
                sp.dma_start(gu[:, :, 1, :], up.rearrange("(k p) f -> p k f", p=128))\
                    .then_inc(raw_loaded[slot], 16)
                sp.dma_start(raw[0:n, slot, 2 * D:3 * D], down).then_inc(raw_loaded[slot], 16)

            def store_combine(group, par, p):
                after(sp, combine_t_copied, known(sp, PAIRS * group + p + 1))
                sp.dma_start(combine_dram[par, :, p * PAIR:(p + 1) * PAIR], combine_t[:, :])\
                    .then_inc(combine_stored, 16)

            def load_spread(e, par, used):
                slot = spread[:, e % RING, :] if e < EXPERTS else spread_sh[:, :]
                loaded = spread_loaded[e % RING] if e < EXPERTS else spread_sh_loaded
                after(sp, weighted, used)
                sp.dma_start(slot, combine_dram[par, e:e + 1, :].broadcast_to([128, GROUP]))\
                    .then_inc(loaded, 16)

            def store_y(group, par):
                for p in range(PAIRS):
                    row, count = known(sp, group * GROUP + p * PAIR), known(sp, PAIRS * group + p + 1)
                    after(sp, y_ready, count)
                    sp.dma_start(out_rows[bass.ds(row, PAIR), :],
                                 x2[:, par, p, :]).then_inc(y_stored, 16)

            def prepare():
                load_x(0, 0, 0)
                load_ctx(0, 0)
                load_x(1, 0, 1)
                for r in range(KC):
                    rows = slice(r * 128, r * 128 + 128)
                    sp.dma_start(wr_raw[:, r, 0:EXPERTS], w_router[rows, :]).then_inc(small_loaded, 16)
                    sp.dma_start(wr_raw[:, r, EXPERTS:COMBINE], w_sh_expert_gate[rows, :])\
                        .then_inc(small_loaded, 16)
                sp.dma_start(gates[:, 0:1], g_xattn.rearrange("(a n) -> a n", a=1).broadcast_to([128, 1]))\
                    .then_inc(small_loaded, 16)
                sp.dma_start(gates[:, 1:2], g_ffn.rearrange("(a n) -> a n", a=1).broadcast_to([128, 1]))\
                    .then_inc(small_loaded, 16)

            def attention(name, p, group, par):
                if name == "load_x":
                    load_x((PAIRS * group + p + 2) % (groups * PAIRS), PAIRS * group + p + 1, p % 2)
                if name == "load_ctx":
                    load_ctx((PAIRS * group + p + 1) % (groups * PAIRS), PAIRS * group + p + 1)
                if name == "weigh":
                    store_combine(group, par, p)

            def body(ffn, par, att):
                a_par = 0 if ffn is None else 1 - par
                for k, (early, late) in enumerate(steps_by_point("SP")):
                    if att is not None:
                        for name, p in early:
                            attention(name, p, att, a_par)
                    if ffn is None and k % 2 == 0:
                        load_weights(k // 2)
                    if ffn is not None and k % 2 == 1 and RING <= (k + 5) // 2 < EXPERTS:
                        e = (k + 5) // 2
                        load_spread(e, par, known(sp, CHUNKS * ffn + e - RING + 1))
                    if ffn is not None and k == 5 and not (isinstance(ffn, int) and ffn == 0):
                        store_y(ffn - 1, 1 - par)
                    if att is not None:
                        for name, p in late:
                            attention(name, p, att, a_par)
                if att is not None:
                    stored = known(sp, 16 * PAIRS * (att + 1))
                    free = [known(sp, CHUNKS * (att - 1) + EXPERTS + e - RING + 1) for e in range(RING)]
                    free.append(known(sp, CHUNKS * att))
                    after(sp, combine_stored, stored)
                    for e in range(RING):
                        load_spread(e, a_par, free[e])
                    load_spread(EXPERTS, a_par, free[RING])

            def drain():
                store_y(groups - 1, (groups - 1) % 2)
                sp.wait_ge(y_stored, 16 * PAIRS * groups)
                sp.wait_ge(combine_stored, 16 * PAIRS * groups)
                for slot in range(2):
                    sp.wait_ge(x_loaded[slot], 16 * (groups * PAIRS // 2 + 1))
                sp.wait_ge(ctx_loaded, 64 * (groups * PAIRS + 1))

            run(sp, prepare, body, drain)

        @block.gpsimd
        def _(pool):
            steps = [0]

            def chain(ins):
                steps[0] += 1
                ins.then_inc(pool_step, 1)
                pool.wait_ge(pool_step, steps[0])

            def prepare():
                nc.gpsimd.memset(x_norm[:, :, :, :], 0.0).then_inc(const_made, 1)
                chain(nc.gpsimd.memset(minus_half[:, :], -0.5))
                chain(nc.gpsimd.memset(ident[:, :], 0.0))
                nc.gpsimd.affine_select(out=ident[:, :], in_=ident[:, :], compare_op=ALU.not_equal,
                                        fill=1.0, base=0, pattern=[[-1, 128]],
                                        channel_multiplier=1).then_inc(const_made, 1)
                chain(nc.gpsimd.memset(head_two[:, :, :], 1.0))
                chain(nc.gpsimd.affine_select(out=head_two[:, :, :], in_=head_two[:, :, :],
                                              compare_op=ALU.is_ge, fill=0.0, base=0,
                                              pattern=[[-SEQ, 2], [-HD, QUARTERS]],
                                              channel_multiplier=1))
                chain(nc.gpsimd.affine_select(out=head_two[:, :, :], in_=head_two[:, :, :],
                                              compare_op=ALU.is_ge, fill=0.0, base=HD - 1,
                                              pattern=[[SEQ, 2], [HD, QUARTERS]],
                                              channel_multiplier=-1))
                chain(nc.gpsimd.tensor_tensor(head_mask[:, :], head_two[:, 0, :], head_two[:, 1, :],
                                              ALU.add))
                chain(nc.gpsimd.memset(causal_f[:, :], 1.0))
                for b in range(2):
                    half = causal_f[b * SEQ:(b + 1) * SEQ, :]
                    last = nc.gpsimd.affine_select(out=half, in_=half, compare_op=ALU.is_ge, fill=0.0,
                                                   base=0, pattern=[[-1, SEQ]],
                                                   channel_multiplier=1)
                    chain(last)
                nc.gpsimd.tensor_copy(causal[:, :], causal_f[:, :]).then_inc(const_made, 1)
                nc.gpsimd.memset(scores[:, :, :], MASKED * HD ** 0.5).then_inc(const_made, 1)
                chain(nc.gpsimd.memset(v_block[:, :, :], 0.0))
                chain(nc.gpsimd.memset(v_block[0:SEQ, :, 4 * HD:4 * HD + 1], 1.0))
                chain(nc.gpsimd.memset(v_block[SEQ:128, :, 4 * HD + 1:4 * HD + 2], 1.0))
                nc.gpsimd.memset(logits[:, EXPERTS:], FAR)
                chain(nc.gpsimd.memset(top_k[:, TOP_K:], FAR))
                for w in (wd_hi, wd_lo):
                    chain(nc.gpsimd.memset(w[SHARED_REST:128, CHUNKS - 1, :].bitcast(f32), 0.0))
                nc.gpsimd.memset(wr_raw[:, :, COMBINE:ROUTES], 0.0).then_inc(const_made, 1)

            def attention(name, p, group):
                pair = PAIRS * group + p
                if name in ("norm", "value"):
                    step, made, spread_ = ((norm1_step, rstd1_made, rstd) if name == "norm" else
                                           (norm2_step, rstd2_made, rstd2))
                    after(pool, step, 3 * (pair + 1))
                    nc.gpsimd.tensor_tensor(spread_[:, :], spread_[:, :], minus_half[:, :], ALU.pow)\
                        .then_inc(made, 1)
                if name == "expand":
                    after(pool, k_copied, pair + 1)
                    for half in range(2):
                        part = slice(2 * half, 2 * half + 2)
                        nc.gpsimd.tensor_tensor(
                            k_block[:, part, :, :],
                            k_t[:, part, :].unsqueeze(2).broadcast_to([128, 2, QUARTERS, SEQ]),
                            head_mask[:, :].unsqueeze(1).unsqueeze(3)
                            .broadcast_to([128, 2, QUARTERS, SEQ]),
                            ALU.mult).then_inc(k_expanded, 1)
                if name == "shift":
                    for half in range(2):
                        part = slice(8 * half, 8 * half + 8)
                        after(pool, maxed, 2 * pair + half + 1)
                        nc.gpsimd.tensor_tensor(
                            probs[:, part, :], scores[:, part, :],
                            row_max[:, part].unsqueeze(2).broadcast_to([128, HEADS // 2, SEQ]),
                            ALU.subtract).then_inc(shifted, 1)

            def weigh_hidden(group, i):
                n = CHUNKS * group + i
                if i < EXPERTS:
                    after(pool, spread_loaded[i % RING], 16 * ((EXPERTS // RING) * group + i // RING + 1))
                    row = spread[:, i % RING, :]
                else:
                    after(pool, spread_sh_loaded, 16 * (group + 1))
                    row = spread_sh[:, :]
                after(pool, upped, n + 1)
                rows = rows_of(i)
                nc.gpsimd.tensor_tensor(act[rows, i % 2, :], act[rows, i % 2, :], row[rows, :],
                                        ALU.mult).then_inc(weighted, 1)

            def body(ffn, par, att):
                for k, (early, late) in enumerate(steps_by_point("Pool")):
                    if att is not None:
                        for name, p in early:
                            attention(name, p, att)
                    if ffn is not None and k % 2 == 1:
                        weigh_hidden(ffn, k // 2)
                    if att is not None:
                        for name, p in late:
                            attention(name, p, att)

            run(pool, prepare, body, lambda: None)

        @block.scalar
        def _(sc):
            def prepare():
                sc.wait_ge(small_loaded, 16 * (2 * KC + 2))
                nc.scalar.activation(gate_tanh[:, :], gates[:, :], ACT.Tanh).then_inc(tanh_made, 1)

            def attention(name, p, group, par):
                pair = PAIRS * group + p
                if name == "values":
                    if isinstance(group, int) and group == 0 and p == 0:
                        sc.wait_ge(const_made, CONSTS)
                    after(sc, ctx_loaded, 64 * (pair + 1))
                    after(sc, valued, 2 * pair)
                    for h in range(2):
                        rows = slice(h * SEQ, (h + 1) * SEQ)
                        dst = v_block[rows, :, 0:4 * HD].rearrange("p j (b h d) -> p j b h d", b=2, h=2)
                        src = ctx_k[rows, :, :, :].rearrange("p c b (j h d) -> p c j b h d", h=2, d=HD)
                        for j in range(2):
                            last = nc.scalar.activation(dst[:, j::2, :, h, :], src[:, :, j, :, h, :],
                                                        ACT.Copy)
                    last.then_inc(v_made, 1)
                if name == "transpose":
                    sc.wait_ge(transposed, pair + 1)
                    nc.scalar.activation(q_t[:, :, :], bank_x.rearrange("p (c t) -> p c t", t=128),
                                         ACT.Copy).then_inc(q_copied, 1)
                if name == "score":
                    for half in range(2):
                        part = slice(8 * half, 8 * half + 8)
                        sc.wait_ge(shifted, 2 * pair + half + 1)
                        nc.scalar.activation(probs[:, part, :], probs[:, part, :], ACT.Exp,
                                             scale=HD ** -0.5).then_inc(probs_made, 1)
                if name == "turn":
                    sc.wait_ge(probs_turned, 2 * pair + 1)
                    nc.scalar.activation(p_t[:, 0:4, :], bank_x.rearrange("p (j t) -> p j t", t=128),
                                         ACT.Copy).then_inc(pt_x_copied, 1)
                if name == "project":
                    sc.wait_ge(x2_turned, pair + 1)
                    nc.scalar.activation(x2t_hi[:, par, :, p * PAIR:(p + 1) * PAIR],
                                         bank_x[:, 0:D].rearrange("p (c t) -> p c t", t=128),
                                         ACT.Copy).then_inc(x2t_hi_made, 1)
                if name == "route":
                    sc.wait_ge(route_step, 4 * pair + 4)
                    nc.scalar.activation(exped[:, :], exponent[:, :], ACT.Exp).then_inc(exps_made, 1)

            def make_hi(n, slot, rows):
                after(sc, weighted, n + 1)
                after(sc, down_done, n - 1)
                nc.scalar.activation(h_hi[rows, slot, :], act[rows, slot, :], ACT.Copy)\
                    .then_inc(hi_ready, 1)

            def weights_hi(i):
                slot = i % STAGING
                sc.wait_ge(raw_loaded[slot], 48 * (i // STAGING + 1))
                n = 128 if i < CHUNKS - 1 else SHARED_REST
                if n < 128:
                    sc.wait_ge(const_made, CONSTS)
                width = 2 * KC * n
                nc.scalar.activation(wgu_hi[:, i, 0:width], raw[:, slot, 0:width], ACT.Copy)
                nc.scalar.activation(wd_hi[0:n, i, :], raw[0:n, slot, 2 * D:3 * D], ACT.Copy)\
                    .then_inc(w_hi_made, 1)

            def body(ffn, par, att):
                first = isinstance(ffn, int) and ffn == 0
                for k, (early, late) in enumerate(steps_by_point("ACT")):
                    if att is not None:
                        for name, p in early:
                            attention(name, p, att, 0 if ffn is None else 1 - par)
                    i = k // 2
                    if ffn is None and k % 2 == 0:
                        weights_hi(i)
                    if ffn is not None and k % 2 == 0:
                        n = CHUNKS * ffn + i
                        after(sc, lo_ready, n - 1)
                        after(sc, gate_ready, n + 1)
                        rows = rows_of(i)
                        nc.scalar.activation(act[rows, i % 2, :], gate_ps[i % 2][rows, :], ACT.Tanh,
                                             scale=0.5).then_inc(tanh_ready, 1)
                    if ffn is not None and k % 2 == 1 and not (first and i == 0):
                        make_hi(CHUNKS * ffn + i - 1, (i - 1) % 2, rows_of((i - 1) % CHUNKS))
                    if att is not None:
                        for name, p in late:
                            attention(name, p, att, 0 if ffn is None else 1 - par)

            run(sc, prepare, body, lambda: make_hi(
                CHUNKS * groups - 1, (CHUNKS - 1) % 2, rows_of(CHUNKS - 1)))

        @block.vector
        def _(ve):
            def prepare():
                ve.wait_ge(small_loaded, 16 * (2 * KC + 2))
                ve.wait_ge(const_made, CONSTS)
                nc.vector.tensor_copy(wr_hi[:, :, :], wr_raw[:, :, :]).then_inc(wr_step, 1)
                ve.wait_ge(wr_step, 1)
                nc.vector.tensor_tensor(wr_lo[:, :, :], wr_raw[:, :, :], wr_hi[:, :, :].bitcast(f32),
                                        ALU.subtract).then_inc(wr_step, 1)

            def attention(name, p, group, par):
                pair = PAIRS * group + p
                if name == "norm":
                    src = x_in[:, p % 2, :]
                    after(ve, x_loaded[p % 2], 16 * (2 * group + p // 2 + 1))
                    nc.vector.bn_stats(stats[:, :], src).then_inc(norm1_step, 1)
                    after(ve, norm1_step, 3 * pair + 1, APART)
                    nc.vector.bn_aggr(moments[:, :], stats[:, :]).then_inc(norm1_step, 1)
                    after(ve, norm1_step, 3 * pair + 2)
                    nc.vector.tensor_scalar(rstd[:, :], moments[:, 1:2], EPS, None, ALU.add)\
                        .then_inc(norm1_step, 1)
                    after(ve, rstd1_made, pair + 1)
                    after(ve, transposed, pair)
                    for b in range(2):
                        rows = slice(b * SEQ, (b + 1) * SEQ)
                        last = nc.vector.tensor_scalar(
                            x_norm[rows, :, b, :], src[rows, :].rearrange("p (c n) -> p c n", c=QUARTERS),
                            moments[rows, 0:1], rstd[rows, :], ALU.subtract, ALU.mult)
                    last.then_inc(queries_normed, 1)
                if name == "transpose":
                    after(ve, transposed, pair + 1)
                    nc.vector.tensor_copy(k_t[:, :, :],
                                          bank_y[:, 0:QUARTERS * SEQ].rearrange("p (c k) -> p c k", k=SEQ))\
                        .then_inc(k_copied, 1)
                if name == "score":
                    mask = causal[:, :].unsqueeze(1).broadcast_to([128, HEADS // 2, SEQ])
                    for half in range(2):
                        part = slice(8 * half, 8 * half + 8)
                        after(ve, scored, 2 * pair + half + 1, APART)
                        nc.vector.copy_predicated(
                            scores[:, part, :], mask,
                            att_ps[:, half, :].rearrange("p (h k) -> p h k", k=SEQ)).then_inc(masked, 1)
                        after(ve, masked, 2 * pair + half + 1)
                        nc.vector.tensor_reduce(row_max[:, part], scores[:, part, :], AX.X, ALU.max)\
                            .then_inc(maxed, 1)
                if name == "turn":
                    after(ve, probs_turned, 2 * pair + 2)
                    nc.vector.tensor_copy(p_t[:, 4:8, :], bank_y.rearrange("p (j t) -> p j t", t=128))\
                        .then_inc(pt_y_copied, 1)
                if name == "value":
                    for half in range(2):
                        part = slice(8 * half, 8 * half + 8)
                        pv = att_ps[:, half, 0:4 * VCOLS].rearrange("p (j v) -> p j v", v=VCOLS)
                        after(ve, valued, 2 * pair + half + 1)
                        nc.vector.reciprocal(inv_sum[:, part].rearrange("p (j h) -> p j h", h=2),
                                             pv[:, :, 4 * HD:VCOLS]).then_inc(inv_made, 1)
                        after(ve, inv_made, 2 * pair + half + 1)
                        for b in range(2):
                            rows = slice(b * SEQ, (b + 1) * SEQ)
                            last = nc.vector.tensor_tensor(
                                attended[rows, half * 128:(half + 1) * 128]
                                .rearrange("p (j h d) -> p j h d", j=4, h=2),
                                pv[rows, :, 2 * HD * b:2 * HD * (b + 1)]
                                .rearrange("p j (h d) -> p j h d", h=2),
                                inv_sum[rows, part].rearrange("p (j h) -> p j h", h=2)
                                .unsqueeze(3).broadcast_to([SEQ, 4, 2, HD]),
                                ALU.mult)
                    last.then_inc(att_scaled, 1)
                    after(ve, att_scaled, pair + 1)
                    if isinstance(group, int) and group == 0:
                        ve.wait_ge(tanh_made, 1)
                    if p == 0:
                        after(ve, y_stored, 16 * PAIRS * (group - 1))
                    nc.vector.scalar_tensor_tensor(
                        out=x2[:, par, p, :], in0=attended[:, :], scalar=gate_tanh[:, 0:1],
                        in1=x_in[:, p % 2, :], op0=ALU.mult, op1=ALU.add).then_inc(x2_made, 1)
                    after(ve, x2_made, pair + 1)
                    src = x2[:, par, p, :]
                    nc.vector.bn_stats(stats2[:, :], src).then_inc(norm2_step, 1)
                    after(ve, norm2_step, 3 * pair + 1, APART)
                    nc.vector.bn_aggr(moments2[:, :], stats2[:, :]).then_inc(norm2_step, 1)
                    after(ve, norm2_step, 3 * pair + 2)
                    nc.vector.tensor_scalar(rstd2[:, :], moments2[:, 1:2], EPS, None, ALU.add)\
                        .then_inc(norm2_step, 1)
                    after(ve, rstd2_made, pair + 1)
                    nc.vector.tensor_scalar(x2_norm[:, :], src, moments2[:, 0:1], rstd2[:, :],
                                            ALU.subtract, ALU.mult).then_inc(x2_normed, 1)
                if name == "project":
                    after(ve, x2t_hi_made, pair + 1)
                    where = slice(p * PAIR, (p + 1) * PAIR)
                    nc.vector.tensor_tensor(x2t_lo[:, par, :, where],
                                            bank_x[:, 0:D].rearrange("p (c t) -> p c t", t=128),
                                            x2t_hi[:, par, :, where].bitcast(f32), ALU.subtract)\
                        .then_inc(x2t_lo_made, 1)
                if name == "route":
                    after(ve, routed, pair + 1)
                    nc.vector.tensor_copy(logits[:, 0:EXPERTS], bank_y[:, 0:EXPERTS])
                    nc.vector.tensor_scalar(exponent[:, EXPERTS:COMBINE], bank_y[:, EXPERTS:COMBINE],
                                            -1.0, None, ALU.mult).then_inc(logits_copied, 1)
                    after(ve, logits_copied, pair + 1, APART)
                    nc.vector.max(top8[:, :], logits[:, 0:EXPERTS]).then_inc(route_step, 1)
                    after(ve, route_step, 4 * pair + 1)
                    nc.vector.tensor_copy(top_k[:, 0:TOP_K], top8[:, 0:TOP_K]).then_inc(route_step, 1)
                    after(ve, route_step, 4 * pair + 2, APART)
                    nc.vector.match_replace(replaced[:, :], top_k[:, :], logits[:, :], -FAR)\
                        .then_inc(route_step, 1)
                    nc.vector.tensor_scalar(exponent[:, 0:EXPERTS], logits[:, 0:EXPERTS], top8[:, 0:1],
                                            None, ALU.subtract).then_inc(route_step, 1)
                    after(ve, route_step, 4 * pair + 4)
                    nc.vector.tensor_tensor(chosen[:, :], replaced[:, 0:EXPERTS], logits[:, 0:EXPERTS],
                                            ALU.not_equal).then_inc(combined, 1)
                if name == "combine":
                    after(ve, combined, 6 * pair + 1)
                    after(ve, exps_made, pair + 1)
                    nc.vector.scalar_tensor_tensor(
                        out=weighed[:, :], in0=exped[:, 0:EXPERTS], scalar=1.0, in1=chosen[:, :],
                        op0=ALU.mult, op1=ALU.mult, accum_out=sums[:, 0:1]).then_inc(combined, 1)
                    nc.vector.tensor_scalar(sums[:, 1:2], exped[:, EXPERTS:COMBINE], 1.0, None, ALU.add)\
                        .then_inc(combined, 1)
                    after(ve, combined, 6 * pair + 3)
                    nc.vector.reciprocal(inv_sums[:, :], sums[:, :]).then_inc(combined, 1)
                    after(ve, combined, 6 * pair + 4)
                    nc.vector.tensor_scalar(combine[:, 0:EXPERTS], weighed[:, :], inv_sums[:, 0:1], 0.5,
                                            ALU.mult, ALU.mult).then_inc(combined, 1)
                    nc.vector.tensor_scalar(combine[:, EXPERTS:COMBINE], inv_sums[:, 1:2], 0.5, None,
                                            ALU.mult).then_inc(combined, 1)
                if name == "weigh":
                    after(ve, combine_turned, pair + 1)
                    after(ve, combine_stored, 16 * pair)
                    nc.vector.tensor_copy(combine_t[:, :], bank_y[0:COMBINE, 0:128])\
                        .then_inc(combine_t_copied, 1)

            def weights_lo(i):
                slot = i % STAGING
                ve.wait_ge(w_hi_made, i + 1)
                n = 128 if i < CHUNKS - 1 else SHARED_REST
                width = 2 * KC * n
                nc.vector.tensor_tensor(wgu_lo[:, i, 0:width], raw[:, slot, 0:width],
                                        wgu_hi[:, i, 0:width].bitcast(f32), ALU.subtract)
                nc.vector.tensor_tensor(wd_lo[0:n, i, :], raw[0:n, slot, 2 * D:3 * D],
                                        wd_hi[0:n, i, :].bitcast(f32), ALU.subtract)\
                    .then_inc(w_lo_made, 1)

            def split_lo(n, slot, rows):
                after(ve, hi_ready, n + 1)
                nc.vector.tensor_tensor(h_lo[rows, slot, :], act[rows, slot, :],
                                        h_hi[rows, slot, :].bitcast(f32), ALU.subtract)\
                    .then_inc(lo_ready, 1)

            def finish_group(group, par):
                after(ve, down_done, CHUNKS * (group + 1))
                for p in range(PAIRS):
                    nc.vector.scalar_tensor_tensor(
                        out=x2[:, par, p, :], in0=out_ps[:, p, :], scalar=gate_tanh[:, 1:2],
                        in1=x2[:, par, p, :], op0=ALU.mult, op1=ALU.add).then_inc(y_ready, 1)

            def body(ffn, par, att):
                first = isinstance(ffn, int) and ffn == 0
                for k, (early, late) in enumerate(steps_by_point("DVE")):
                    n = None if ffn is None else CHUNKS * ffn + k // 2
                    if k == 4 and ffn is not None and not first:
                        finish_group(ffn - 1, 1 - par)
                    if att is not None:
                        for name, p in early:
                            attention(name, p, att, 0 if ffn is None else 1 - par)
                    i = k // 2
                    if ffn is not None and k % 2 == 1 and not (first and i == 0):
                        split_lo(n - 1, (i - 1) % 2, rows_of((i - 1) % CHUNKS))
                    if ffn is None and k % 2 == 0:
                        weights_lo(i)
                    if ffn is not None and k % 2 == 0:
                        rows = rows_of(i)
                        a, gate, up = act[rows, i % 2, :], gate_ps[i % 2][rows, :], up_ps[i % 2][rows, :]
                        after(ve, tanh_ready, n + 1)
                        nc.vector.scalar_tensor_tensor(out=a, in0=a, scalar=1.0, in1=gate,
                                                       op0=ALU.add, op1=ALU.mult).then_inc(gated, 1)
                        if i < CHUNKS - 1:
                            after(ve, up_ready, (CHUNKS - 1) * ffn + i + 1)
                        else:
                            up = gate_ps[i % 2][SHARED_REST:2 * SHARED_REST, :]
                        after(ve, gated, n + 1)
                        nc.vector.tensor_tensor(a, a, up, ALU.mult).then_inc(upped, 1)
                    if att is not None:
                        for name, p in late:
                            attention(name, p, att, 0 if ffn is None else 1 - par)

            def drain():
                split_lo(CHUNKS * groups - 1, (CHUNKS - 1) % 2, rows_of(CHUNKS - 1))
                finish_group(groups - 1, (groups - 1) % 2)

            run(ve, prepare, body, drain)

        @block.tensor
        def _(te):
            def three(out_ap, a_hi, a_lo, b_hi, b_lo, first, last, check=False):
                nc.tensor.matmul(out_ap, a_hi, b_hi, start=first, stop=False, skip_group_check=check)
                nc.tensor.matmul(out_ap, a_hi, b_lo, start=False, stop=False, skip_group_check=check)
                return nc.tensor.matmul(out_ap, a_lo, b_hi, start=False, stop=last,
                                        skip_group_check=check)

            def attention(name, p, group, par):
                pair = PAIRS * group + p
                if name == "transpose":
                    after(te, queries_normed, pair + 1)
                    after(te, ctx_loaded, 64 * (pair + 1))
                    if p:
                        after(te, att_scaled, pair)
                        after(te, combine_t_copied, pair - 1)
                    else:
                        after(te, x2t_lo_made, pair)
                        after(te, combine_t_copied, pair)
                    for c in range(QUARTERS):
                        nc.tensor.transpose(bank_x[:, c * 128:(c + 1) * 128],
                                            x_norm[:, c, :, :].rearrange("p b n -> p (b n)"), ident[:, :])
                    for c in range(QUARTERS):
                        last = nc.tensor.transpose(bank_y[:, c * SEQ:(c + 1) * SEQ],
                                                   ctx_k[0:SEQ, c, :, :].rearrange("p b n -> p (b n)"),
                                                   ident[0:SEQ, 0:SEQ])
                    last.then_inc(transposed, 1)
                if name == "score":
                    after(te, q_copied, pair + 1)
                    after(te, x2t_lo_made, pair if p else 0)
                    for half in range(2):
                        after(te, k_expanded, 2 * pair + half + 1)
                        for c in (2 * half, 2 * half + 1):
                            last = nc.tensor.matmul(
                                att_ps[:, half, (c % 2) * 256:(c % 2 + 1) * 256], q_t[:, c, :],
                                k_block[:, c, :, :].rearrange("p h k -> p (h k)"), start=True,
                                stop=True)
                        last.then_inc(scored, 1)
                if name == "turn":
                    after(te, logits_copied, pair if p else 0)
                    for half in range(2):
                        after(te, probs_made, 2 * pair + half + 1)
                        for j in range(4 * half, 4 * half + 4):
                            last = nc.tensor.transpose(
                                att_ps[:, half, (j % 4) * 128:(j % 4 + 1) * 128],
                                probs[:, 2 * j:2 * j + 2, :].rearrange("p h k -> p (h k)"), ident[:, :])
                        last.then_inc(probs_turned, 1)
                if name == "value":
                    after(te, v_made, pair + 1)
                    for half, copied in enumerate((pt_x_copied, pt_y_copied)):
                        after(te, copied, pair + 1)
                        for j in range(4 * half, 4 * half + 4):
                            last = nc.tensor.matmul(
                                att_ps[:, half, (j % 4) * VCOLS:(j % 4 + 1) * VCOLS], p_t[:, j, :],
                                v_block[:, j, :], start=True, stop=True)
                        last.then_inc(valued, 1)
                if name == "project":
                    after(te, x2_normed, pair + 1)
                    if p < PAIRS - 1:
                        after(te, q_copied, pair + 2)
                    for c in range(KC):
                        last = nc.tensor.transpose(bank_x[:, c * 128:(c + 1) * 128],
                                                   x2_norm[:, c * 128:(c + 1) * 128], ident[:, :])
                    last.then_inc(x2_turned, 1)
                if name == "route":
                    after(te, x2t_lo_made, pair + 1)
                    if p < PAIRS - 1:
                        after(te, masked, 2 * (pair + 2))
                    where = slice(p * PAIR, (p + 1) * PAIR)
                    for c in range(KC):
                        last = three(bank_y[:, 0:ROUTES], x2t_hi[:, par, c, where],
                                     x2t_lo[:, par, c, where], wr_hi[:, c, :], wr_lo[:, c, :],
                                     c == 0, c == KC - 1)
                    last.then_inc(routed, 1)
                if name == "weigh":
                    after(te, combined, 6 * (pair + 1))
                    if p < PAIRS - 1:
                        after(te, att_scaled, pair + 2)
                    nc.tensor.transpose(bank_y[0:COMBINE, 0:128], combine[:, :], ident[:, :])\
                        .then_inc(combine_turned, 1)

            def gate_up(group, par, i):
                n = CHUNKS * group + i
                after(te, upped if i == 1 else gated, n - 1)
                if isinstance(group, int) and group == 0:
                    te.wait_ge(w_lo_made, i + 1)
                hi, lo = gate_up_of(wgu_hi[:, i, :], i), gate_up_of(wgu_lo[:, i, :], i)
                if i == CHUNKS - 1:
                    after(te, upped, n - 1)
                    for c in range(KC):
                        last = three(gate_ps[i % 2][:, :], hi[:, c, :, :].rearrange("p s f -> p (s f)"),
                                     lo[:, c, :, :].rearrange("p s f -> p (s f)"),
                                     x2t_hi[:, par, c, :], x2t_lo[:, par, c, :], c == 0, c == KC - 1)
                    last.then_inc(gate_ready, 1)
                    return
                for s, bank, ready in ((0, gate_ps, gate_ready), (1, up_ps, up_ready)):
                    if s:
                        after(te, upped, n - 1)
                    for c in range(KC):
                        last = three(bank[i % 2][:, :], hi[:, c, s, :], lo[:, c, s, :],
                                     x2t_hi[:, par, c, :], x2t_lo[:, par, c, :], c == 0, c == KC - 1)
                    last.then_inc(ready, 1)

            def down(group, i):
                n = CHUNKS * group + i
                after(te, lo_ready, n + 1)
                if i == 0:
                    after(te, y_ready, PAIRS * group)
                for p in range(PAIRS):
                    where = slice(p * PAIR, (p + 1) * PAIR)
                    last = three(out_ps[:, p, :], h_hi[:, i % 2, where], h_lo[:, i % 2, where],
                                 wd_hi[:, i, :], wd_lo[:, i, :], i == 0 and p % 2 == 0,
                                 i == CHUNKS - 1, True)
                last.then_inc(down_done, 1)

            def prepare():
                te.wait_ge(const_made, CONSTS)
                te.wait_ge(wr_step, 2)

            def body(ffn, par, att):
                first = isinstance(ffn, int) and ffn == 0
                for k, (early, late) in enumerate(steps_by_point("PE")):
                    if att is not None:
                        for name, p in early:
                            attention(name, p, att, 0 if ffn is None else 1 - par)
                    i = k // 2
                    if ffn is not None and k % 2 == 0:
                        gate_up(ffn, par, i)
                    if ffn is not None and k % 2 == 1:
                        if i >= 2:
                            down(ffn, i - 2)
                        elif not first:
                            down(ffn - 1, CHUNKS + i - 2)
                    if att is not None:
                        for name, p in late:
                            attention(name, p, att, 0 if ffn is None else 1 - par)

            def drain():
                down(groups - 1, CHUNKS - 2)
                down(groups - 1, CHUNKS - 1)

            run(te, prepare, body, drain)


_INS = ["x", "ctx_2048", "g_xattn", "g_ffn", "L0_ffn_w_router", "L0_ffn_w_gate", "L0_ffn_w_up",
        "L0_ffn_w_down", "L0_ffn_w_sh_gate", "L0_ffn_w_sh_up", "L0_ffn_w_sh_down",
        "L0_ffn_w_sh_expert_gate"]


def kernel(**inputs):
    import numpy as _np
    import concourse.bacc as _bacc
    from concourse import mybir as _mybir
    from concourse.bass_utils import run_bass_kernel_spmd as _run

    nc = _bacc.Bacc("TRN2", target_bir_lowering=False, num_devices=1, dynamic_dma_scratch_size=1024)
    arrays, args = {}, []
    for name in _INS:
        a = _np.ascontiguousarray(inputs[name])
        arrays[f"in_{name}"] = a
        args.append(nc.dram_tensor(f"in_{name}", a.shape, _mybir.dt.from_np(a.dtype),
                                   kind="ExternalInput").ap())
    shape = inputs["x"].shape
    args.append(nc.dram_tensor("out_0", shape, _mybir.dt.float32, kind="ExternalOutput").ap())
    flamingo_block(nc, *args)
    r = _run(nc, [arrays], core_ids=[0])
    return r.results[0]["out_0"]
```

```python
import concourse.bass as bass
from concourse import mybir
from contextlib import ExitStack

D = 256
KC = D // 128
SEQ = 64
HEADS, HD = 16, 16
EXPERTS, TOP_K = 16, 4
SHARED = 704
SHARED_CHUNKS = -(-SHARED // 128)
SHARED_REST = SHARED - 128 * (SHARED_CHUNKS - 1)
CHUNKS = EXPERTS + SHARED_CHUNKS
PAIR = 2 * SEQ
PAIRS = 4
GROUP = PAIRS * PAIR
QUARTERS = 4
POINTS = 2 * CHUNKS
COMBINE = EXPERTS + 1
RING = 4
STAGING = 4
VCOLS = 2 * 2 * HD + 2
MASKED = -10000.0
EPS = 1e-5
FAR = 3.0e38

STARTS = (2, 11, 20, 29)
STEPS = {
    "PE": {"transpose": (0, 0), "score": (2, 2), "turn": (5, 5), "value": (6, 6),
           "project": (10, 8), "route": (12, 10), "weigh": (16, 12)},
    "SP": {"load_x": (7, 7), "load_ctx": (1, 1), "weigh": (16, 12)},
    "Pool": {"norm": (-6, -6), "expand": (0, 0), "shift": (3, 3), "value": (6.5, 6.5)},
    "ACT": {"values": (-2.5, -2.5), "transpose": (0, 0), "score": (3.5, 3.5), "score2": (3.5, 3.5),
            "turn": (5, 5), "project": (10, 8), "route": (12.5, 10.5)},
    "DVE": {"norm": (-6, -6), "center": (-5, -5), "transpose": (0, 0), "score": (2, 2),
            "score2": (2, 2), "turn": (5, 5), "value": (6, 6), "value2": (6, 6), "center2": (7, 7),
            "project": (10, 8), "route": (12, 10), "choose": (12, 10), "combine": (13, 11),
            "weigh": (16, 12)},
}
WEIGHTS_FROM, WEIGHTS_EVERY = 4, 3
STARTS_ALONE = (1, 9, 17, 25)
STEPS_ALONE = {
    "PE": {"transpose": (-2, -3), "score": (1, 0), "turn": (4, 3), "value": (6.5, 7),
           "project": (10.5, 9), "route": (11, 12.5), "weigh": (13, 14.5)},
    "SP": {"load_x": (9.5, 11.5), "load_ctx": (-2, 1), "weigh": (16.5, 14.5)},
    "Pool": {"norm": (-2, -2), "expand": (1.5, -0.5), "shift": (6, 6), "value": (10.5, 8)},
    "ACT": {"values": (1.5, 2.5), "transpose": (0.5, 2), "score": (4.5, 3.5), "score2": (4.5, 3.5),
            "turn": (6, 6), "project": (11.5, 10.5), "route": (12, 12)},
    "DVE": {"norm": (-4, -4), "center": (-3.5, -3), "transpose": (-0.5, -0.5), "score": (3, 1),
            "score2": (3, 2.5), "turn": (6.5, 6.5), "value": (9, 6.5), "value2": (9, 9),
            "center2": (9, 9), "project": (10.5, 11), "route": (12, 11.5), "choose": (12, 12),
            "combine": (12.5, 12.5), "weigh": (14, 15)},
}


def steps_by_point(engine, alone):
    starts, steps = (STARTS_ALONE, STEPS_ALONE) if alone else (STARTS, STEPS)
    at = [([], []) for _ in range(POINTS)]
    for p in range(PAIRS):
        for order, (name, offsets) in enumerate(steps[engine].items()):
            when = max(0, starts[p] + offsets[p == PAIRS - 1])
            point = min(int(when), POINTS - 1)
            at[point][when != point].append((when, p, order, name))
    return [[[(name, p) for _, p, _, name in sorted(part)] for part in parts]
            for parts in at]


def weights_at(k, ffn, ahead=0):
    alone, first = ffn is None, isinstance(ffn, int) and ffn == 0
    k += 0 if alone else POINTS
    return [i for i in range(ahead, CHUNKS) if (alone or first)
            and k == int(WEIGHTS_FROM + WEIGHTS_EVERY * (i - ahead))]


def known(eng, value):
    return value if isinstance(value, int) else eng.snap(eng.to_reg(value))


def after(eng, sem, count, apart=None):
    if apart is not None and not isinstance(count, int):
        count = known(eng, count)
        eng.wait_ge(*apart)
    if not isinstance(count, int) or count > 0:
        eng.wait_ge(sem, count)


def flamingo_block(nc, x, ctx_in, g_xattn, g_ffn, w_router, w_gate, w_up, w_down, w_sh_gate, w_sh_up,
                   w_sh_down, w_sh_expert_gate, out):
    f32, f32r, u8 = mybir.dt.float32, mybir.dt.float32r, mybir.dt.uint8
    ALU, ACT, AX = mybir.AluOpType, mybir.ActivationFunctionType, mybir.AxisListType

    tokens = x.shape[0] * x.shape[1]
    groups = tokens // GROUP
    x_rows = x.rearrange("b s d -> (b s) d")
    out_rows = out.rearrange("b s d -> (b s) d")
    combine_dram = nc.dram_tensor("combine_rows", (2, COMBINE, GROUP), f32, kind="Internal").ap()

    ctx = ExitStack()
    with ctx:
        def sb(name, shape, dt=f32):
            return ctx.enter_context(nc.sbuf_tensor(name, shape, dt))

        def ps(name, shape):
            return ctx.enter_context(nc.psum_tensor(name, shape, f32))

        def sem(name):
            return ctx.enter_context(nc.semaphore(name))

        wgu_hi = sb("wgu_hi", [128, CHUNKS, 2 * D], f32r)
        wgu_lo = sb("wgu_lo", [128, CHUNKS, 2 * D], f32r)
        wd_hi = sb("wd_hi", [128, CHUNKS, D], f32r)
        wd_lo = sb("wd_lo", [128, CHUNKS, D], f32r)
        w_route = sb("w_route", [128, KC, COMBINE])
        raw = sb("raw", [128, STAGING, 3 * D])
        ident = sb("ident", [128, 128])
        head_mask = sb("head_mask", [128, QUARTERS])
        head_two = sb("head_two", [128, 2, QUARTERS])
        causal_f = sb("causal_f", [128, SEQ])
        causal = sb("causal", [128, SEQ], u8)
        minus_half = sb("minus_half", [128, 1])
        gates = sb("gates", [128, 2])
        gate_tanh = sb("gate_tanh", [128, 2])
        x_in = sb("x_in", [128, PAIRS, D])
        ctx_k = sb("ctx_k", [128, QUARTERS, 2, SEQ])
        stats = sb("stats", [128, 6])
        moments = sb("moments", [128, 2])
        rstd = sb("rstd", [128, 1])
        stats2 = sb("stats2", [128, 6])
        moments2 = sb("moments2", [128, 2])
        rstd2 = sb("rstd2", [128, 1])
        x_norm = sb("x_norm", [128, QUARTERS, 2, SEQ])
        q_t = sb("q_t", [128, QUARTERS, 128])
        k_t = sb("k_t", [128, QUARTERS, SEQ])
        k_block = sb("k_block", [128, QUARTERS, QUARTERS, SEQ])
        scores = sb("scores", [128, HEADS, SEQ])
        row_max = sb("row_max", [128, HEADS])
        probs = sb("probs", [128, HEADS, SEQ])
        v_block = sb("v_block", [128, HEADS // 2, VCOLS])
        inv_sum = sb("inv_sum", [128, HEADS])
        attended = sb("attended", [128, D])
        x2 = sb("x2", [128, 2, PAIRS, D])
        x2_norm = sb("x2_norm", [128, D])
        x2t = sb("x2t", [128, KC, PAIR])
        x2t_hi = sb("x2t_hi", [128, 2, KC, GROUP], f32r)
        x2t_lo = sb("x2t_lo", [128, 2, KC, GROUP], f32r)
        logits = sb("logits", [128, EXPERTS + 8 - TOP_K])
        top8 = sb("top8", [128, 8])
        top_k = sb("top_k", [128, 8])
        replaced = sb("replaced", [128, EXPERTS + 8 - TOP_K])
        exponent = sb("exponent", [128, COMBINE])
        exped = sb("exped", [128, COMBINE])
        chosen = sb("chosen", [128, EXPERTS])
        weighed = sb("weighed", [128, EXPERTS])
        sums = sb("sums", [128, 2])
        inv_sums = sb("inv_sums", [128, 2])
        combine = sb("combine", [128, COMBINE])
        combine_t = sb("combine_t", [COMBINE, 128])
        spread = sb("spread", [128, RING, GROUP])
        spread_sh = sb("spread_sh", [128, GROUP])
        act = sb("act", [128, 2, GROUP])
        p_t_of = {False: k_block[:, :, :, :].rearrange("p a b c -> p (a b c)")
                  .rearrange("p (j t) -> p j t", t=128),
                  True: act[:, :, :].rearrange("p s t -> p (s t)").rearrange("p (j t) -> p j t", t=128)}
        h_hi = sb("h_hi", [128, 2, GROUP], f32r)
        h_lo = sb("h_lo", [128, 2, GROUP], f32r)

        gate_ps = [ps(f"gate_ps{i}", [128, GROUP]) for i in range(2)]
        up_ps = [ps(f"up_ps{i}", [128, GROUP]) for i in range(2)]
        out_ps = ps("out_ps", [128, PAIRS, D])
        att_ps = ps("att_ps", [128, 2, 512])

        def att_banks(alone):
            x, y = att_ps[:, 0, :], att_ps[:, 1, :]
            if not alone:
                return {"queries": x, "keys": y, "scores": (x, y), "turned": (x, y),
                        "values": (x, y), "x2": x, "logits": y, "combine": y}
            v = [out_ps[:, 2 * b:2 * b + 2, :].rearrange("p a d -> p (a d)") for b in range(2)]
            return {"queries": gate_ps[0][:, :], "keys": gate_ps[1][:, 0:256], "scores": (x, y),
                    "turned": (up_ps[0][:, :], up_ps[1][:, :]), "values": v,
                    "x2": gate_ps[1][:, 256:512], "logits": v[0][:, 384:512],
                    "combine": v[1][:, 384:512]}

        raw_loaded = [sem(f"raw_loaded{i}") for i in range(STAGING)]
        small_loaded = sem("small_loaded")
        x_loaded = [sem(f"x_loaded{i}") for i in range(PAIRS)]
        ctx_loaded = sem("ctx_loaded")
        const_made = sem("const_made")
        pool_step = sem("pool_step")
        tanh_made = sem("tanh_made")
        w_hi_made, w_lo_made = sem("w_hi_made"), sem("w_lo_made")
        norm1_step, queries_normed = sem("norm1_step"), sem("queries_normed")
        rstd1_made, rstd2_made = sem("rstd1_made"), sem("rstd2_made")
        transposed = sem("transposed")
        q_copied, k_copied, k_expanded = sem("q_copied"), sem("k_copied"), sem("k_expanded")
        scored, masked, maxed, shifted, probs_made = (sem(n) for n in (
            "scored", "masked", "maxed", "shifted", "probs_made"))
        probs_turned, pt_x_copied, pt_y_copied = (sem(n) for n in (
            "probs_turned", "pt_x_copied", "pt_y_copied"))
        v_made, valued, inv_made, att_scaled, x2_made = (sem(n) for n in (
            "v_made", "valued", "inv_made", "att_scaled", "x2_made"))
        norm2_step, x2_normed, x2_turned, x2t_hi_made, x2t_lo_made = (sem(n) for n in (
            "norm2_step", "x2_normed", "x2_turned", "x2t_hi_made", "x2t_lo_made"))
        routed, logits_copied, route_step, exps_made, combined = (sem(n) for n in (
            "routed", "logits_copied", "route_step", "exps_made", "combined"))
        combine_turned, combine_t_copied, combine_stored = (sem(n) for n in (
            "combine_turned", "combine_t_copied", "combine_stored"))
        spread_loaded = [sem(f"spread_loaded{i}") for i in range(RING)]
        spread_sh_loaded = sem("spread_sh_loaded")
        gate_ready, up_ready, tanh_ready, gated, upped, weighted, hi_ready, lo_ready, down_done = (
            sem(n) for n in ("gate_ready", "up_ready", "tanh_ready", "gated", "upped", "weighted",
                             "hi_ready", "lo_ready", "down_done"))
        y_ready, y_stored = sem("y_ready"), sem("y_stored")
        CONSTS = 4
        APART = (const_made, CONSTS)

        def rows_of(i):
            return slice(0, 128 if i < CHUNKS - 1 else SHARED_REST)

        def gate_up_of(flat, i):
            n = 128 if i < CHUNKS - 1 else SHARED_REST
            return flat[:, 0:2 * KC * n].rearrange("p (k s f) -> p k s f", k=KC, s=2)

        def run(eng, prepare, body, drain):
            prepare()
            body(None, None, 0)
            body(0, 0, 1)
            with eng.Fori(0, (groups - 2) // 2) as n:
                body(2 * n + 1, 1, 2 * n + 2)
                body(2 * n + 2, 0, 2 * n + 3)
            body(groups - 1, 1, None)
            drain()

        block = ctx.enter_context(nc.Block())

        @block.sync
        def _(sp):
            def load_x(pair, before, slot):
                row, used = known(sp, pair * PAIR), known(sp, before)
                after(sp, x2_made, used)
                sp.dma_start(x_in[:, slot, :], x_rows[bass.ds(row, PAIR), :])\
                    .then_inc(x_loaded[slot], 16)

            def load_ctx(pair, before):
                before = known(sp, before)
                batch = [known(sp, pair * 2 + b) for b in range(2)]
                after(sp, transposed, before)
                after(sp, v_made, before)
                for b in range(2):
                    src = ctx_in[bass.ds(batch[b], 1), :, :]\
                        .rearrange("b k (c n) -> (b k) c n", c=QUARTERS)
                    for copy in range(2):
                        rows = slice(copy * SEQ, (copy + 1) * SEQ)
                        sp.dma_start(ctx_k[rows, :, b, :], src).then_inc(ctx_loaded, 16)

            def load_weights(i):
                slot = i % STAGING
                after(sp, w_lo_made, i - STAGING + 1)
                after(sp, w_hi_made, i - STAGING + 1)
                gu = gate_up_of(raw[:, slot, 0:2 * D], i)
                if i < EXPERTS:
                    gate, up, down = w_gate[i, :, :], w_up[i, :, :], w_down[i, :, :]
                    n = 128
                else:
                    f0 = (i - EXPERTS) * 128
                    n = min(128, SHARED - f0)
                    gate, up = w_sh_gate[:, f0:f0 + n], w_sh_up[:, f0:f0 + n]
                    down = w_sh_down[f0:f0 + n, :]
                sp.dma_start(gu[:, :, 0, :], gate.rearrange("(k p) f -> p k f", p=128))\
                    .then_inc(raw_loaded[slot], 16)
                sp.dma_start(gu[:, :, 1, :], up.rearrange("(k p) f -> p k f", p=128))\
                    .then_inc(raw_loaded[slot], 16)
                sp.dma_start(raw[0:n, slot, 2 * D:3 * D], down).then_inc(raw_loaded[slot], 16)

            def store_combine(group, par, p):
                after(sp, combine_t_copied, known(sp, PAIRS * group + p + 1))
                sp.dma_start(combine_dram[par, :, p * PAIR:(p + 1) * PAIR], combine_t[:, :])\
                    .then_inc(combine_stored, 16)

            def load_spread(e, par, used):
                slot = spread[:, e % RING, :] if e < EXPERTS else spread_sh[:, :]
                loaded = spread_loaded[e % RING] if e < EXPERTS else spread_sh_loaded
                after(sp, weighted, used)
                sp.dma_start(slot, combine_dram[par, e:e + 1, :].broadcast_to([128, GROUP]))\
                    .then_inc(loaded, 16)

            def store_y(group, par):
                for p in range(PAIRS):
                    row, count = known(sp, group * GROUP + p * PAIR), known(sp, PAIRS * group + p + 1)
                    after(sp, y_ready, count)
                    sp.dma_start(out_rows[bass.ds(row, PAIR), :],
                                 x2[:, par, p, :]).then_inc(y_stored, 16)

            def prepare():
                load_x(0, 0, 0)
                load_ctx(0, 0)
                for p in range(1, PAIRS):
                    load_x(p, 0, p)
                for r in range(KC):
                    rows = slice(r * 128, r * 128 + 128)
                    sp.dma_start(w_route[:, r, 0:EXPERTS], w_router[rows, :]).then_inc(small_loaded, 16)
                    sp.dma_start(w_route[:, r, EXPERTS:COMBINE], w_sh_expert_gate[rows, :])\
                        .then_inc(small_loaded, 16)
                sp.dma_start(gates[:, 0:1], g_xattn.rearrange("(a n) -> a n", a=1).broadcast_to([128, 1]))\
                    .then_inc(small_loaded, 16)
                sp.dma_start(gates[:, 1:2], g_ffn.rearrange("(a n) -> a n", a=1).broadcast_to([128, 1]))\
                    .then_inc(small_loaded, 16)
                for i in range(STAGING):
                    load_weights(i)

            def attention(name, p, group, par):
                if name == "load_x":
                    load_x((PAIRS * group + p + PAIRS) % (groups * PAIRS), PAIRS * group + p + 1, p)
                if name == "load_ctx":
                    load_ctx((PAIRS * group + p + 1) % (groups * PAIRS), PAIRS * group + p + 1)
                if name == "weigh":
                    store_combine(group, par, p)

            def body(ffn, par, att):
                a_par = 0 if ffn is None else 1 - par
                for k, (early, late) in enumerate(steps_by_point("SP", ffn is None)):
                    if att is not None:
                        for name, p in early:
                            attention(name, p, att, a_par)
                    for i in weights_at(k, ffn, ahead=STAGING):
                        load_weights(i)
                    if ffn is not None and k % 2 == 1 and RING <= (k + 5) // 2 < EXPERTS:
                        e = (k + 5) // 2
                        load_spread(e, par, known(sp, CHUNKS * ffn + e - RING + 1))
                    if ffn is not None and k == 5 and not (isinstance(ffn, int) and ffn == 0):
                        store_y(ffn - 1, 1 - par)
                    if att is not None:
                        for name, p in late:
                            attention(name, p, att, a_par)
                if att is not None:
                    stored = known(sp, 16 * PAIRS * (att + 1))
                    free = [known(sp, CHUNKS * (att - 1) + EXPERTS + e - RING + 1) for e in range(RING)]
                    free.append(known(sp, CHUNKS * att))
                    after(sp, combine_stored, stored)
                    for e in range(RING):
                        load_spread(e, a_par, free[e])
                    load_spread(EXPERTS, a_par, free[RING])

            def drain():
                store_y(groups - 1, (groups - 1) % 2)
                sp.wait_ge(y_stored, 16 * PAIRS * groups)
                sp.wait_ge(combine_stored, 16 * PAIRS * groups)
                for p in range(PAIRS):
                    sp.wait_ge(x_loaded[p], 16 * (groups + 1))
                sp.wait_ge(ctx_loaded, 64 * (groups * PAIRS + 1))

            run(sp, prepare, body, drain)

        @block.gpsimd
        def _(pool):
            steps = [0]

            def chain(ins):
                steps[0] += 1
                ins.then_inc(pool_step, 1)
                pool.wait_ge(pool_step, steps[0])

            def prepare():
                nc.gpsimd.memset(x_norm[:, :, :, :], 0.0).then_inc(const_made, 1)
                chain(nc.gpsimd.memset(minus_half[:, :], -0.5))
                chain(nc.gpsimd.memset(ident[:, :], 0.0))
                nc.gpsimd.affine_select(out=ident[:, :], in_=ident[:, :], compare_op=ALU.not_equal,
                                        fill=1.0, base=0, pattern=[[-1, 128]],
                                        channel_multiplier=1).then_inc(const_made, 1)
                chain(nc.gpsimd.memset(head_two[:, :, :], 1.0))
                chain(nc.gpsimd.affine_select(out=head_two[:, :, :], in_=head_two[:, :, :],
                                              compare_op=ALU.is_ge, fill=0.0, base=0,
                                              pattern=[[-SEQ, 2], [-HD, QUARTERS]],
                                              channel_multiplier=1))
                chain(nc.gpsimd.affine_select(out=head_two[:, :, :], in_=head_two[:, :, :],
                                              compare_op=ALU.is_ge, fill=0.0, base=HD - 1,
                                              pattern=[[SEQ, 2], [HD, QUARTERS]],
                                              channel_multiplier=-1))
                chain(nc.gpsimd.tensor_tensor(head_mask[:, :], head_two[:, 0, :], head_two[:, 1, :],
                                              ALU.add))
                chain(nc.gpsimd.memset(causal_f[:, :], 1.0))
                for b in range(2):
                    half = causal_f[b * SEQ:(b + 1) * SEQ, :]
                    last = nc.gpsimd.affine_select(out=half, in_=half, compare_op=ALU.is_ge, fill=0.0,
                                                   base=0, pattern=[[-1, SEQ]],
                                                   channel_multiplier=1)
                    chain(last)

            def prepare_more():
                nc.gpsimd.memset(scores[:, :, :], MASKED * HD ** 0.5).then_inc(const_made, 1)
                chain(nc.gpsimd.memset(v_block[:, :, :], 0.0))
                chain(nc.gpsimd.memset(v_block[0:SEQ, :, 4 * HD:4 * HD + 1], 1.0))
                chain(nc.gpsimd.memset(v_block[SEQ:128, :, 4 * HD + 1:4 * HD + 2], 1.0))
                nc.gpsimd.memset(logits[:, EXPERTS:], FAR)
                chain(nc.gpsimd.memset(top_k[:, TOP_K:], FAR))
                for w in (wd_hi, wd_lo):
                    chain(nc.gpsimd.memset(w[SHARED_REST:128, CHUNKS - 1, :].bitcast(f32), 0.0))
                nc.gpsimd.tensor_copy(causal[:, :], causal_f[:, :]).then_inc(const_made, 1)

            def attention(name, p, group, alone):
                pair = PAIRS * group + p
                if name in ("norm", "value"):
                    step, made, spread_ = ((norm1_step, rstd1_made, rstd) if name == "norm" else
                                           (norm2_step, rstd2_made, rstd2))
                    after(pool, step, 3 * (pair + 1))
                    nc.gpsimd.tensor_tensor(spread_[:, :], spread_[:, :], minus_half[:, :], ALU.pow)\
                        .then_inc(made, 1)
                if name == "expand":
                    after(pool, k_copied, pair + 1)
                    for half in range(2):
                        part = slice(2 * half, 2 * half + 2)
                        nc.gpsimd.tensor_tensor(
                            k_block[:, part, :, :],
                            k_t[:, part, :].unsqueeze(2).broadcast_to([128, 2, QUARTERS, SEQ]),
                            head_mask[:, :].unsqueeze(1).unsqueeze(3)
                            .broadcast_to([128, 2, QUARTERS, SEQ]),
                            ALU.mult).then_inc(k_expanded, 1)
                if name == "shift":
                    for half in range(2):
                        part = slice(8 * half, 8 * half + 8)
                        if alone:
                            after(pool, probs_turned, 2 * pair - 1 + half)
                        after(pool, maxed, 2 * pair + half + 1)
                        nc.gpsimd.tensor_tensor(
                            probs[:, part, :], scores[:, part, :],
                            row_max[:, part].unsqueeze(2).broadcast_to([128, HEADS // 2, SEQ]),
                            ALU.subtract).then_inc(shifted, 1)

            def weigh_hidden(group, i):
                n = CHUNKS * group + i
                if i < EXPERTS:
                    after(pool, spread_loaded[i % RING], 16 * ((EXPERTS // RING) * group + i // RING + 1))
                    row = spread[:, i % RING, :]
                else:
                    after(pool, spread_sh_loaded, 16 * (group + 1))
                    row = spread_sh[:, :]
                after(pool, upped, n + 1)
                rows = rows_of(i)
                nc.gpsimd.tensor_tensor(act[rows, i % 2, :], act[rows, i % 2, :], row[rows, :],
                                        ALU.mult).then_inc(weighted, 1)

            def body(ffn, par, att):
                for k, (early, late) in enumerate(steps_by_point("Pool", ffn is None)):
                    if att is not None:
                        for name, p in early:
                            attention(name, p, att, ffn is None)
                    if ffn is None and k == 0:
                        prepare_more()
                    if ffn is not None and k % 2 == 1:
                        weigh_hidden(ffn, k // 2)
                    if att is not None:
                        for name, p in late:
                            attention(name, p, att, ffn is None)

            run(pool, prepare, body, lambda: None)

        @block.scalar
        def _(sc):
            def gates_tanh():
                sc.wait_ge(small_loaded, 16 * (2 * KC + 2))
                nc.scalar.activation(gate_tanh[:, :], gates[:, :], ACT.Tanh).then_inc(tanh_made, 1)

            def attention(name, p, group, par, alone):
                pair = PAIRS * group + p
                bank, p_t = att_banks(alone), p_t_of[alone]
                if name == "values":
                    if isinstance(group, int) and group == 0 and p == 0:
                        sc.wait_ge(const_made, CONSTS)
                    after(sc, ctx_loaded, 64 * (pair + 1))
                    after(sc, valued, 2 * pair)
                    for h in range(2):
                        rows = slice(h * SEQ, (h + 1) * SEQ)
                        dst = v_block[rows, :, 0:4 * HD].rearrange("p j (b h d) -> p j b h d", b=2, h=2)
                        src = ctx_k[rows, :, :, :].rearrange("p c b (j h d) -> p c j b h d", h=2, d=HD)
                        for j in range(2):
                            last = nc.scalar.activation(dst[:, j::2, :, h, :], src[:, :, j, :, h, :],
                                                        ACT.Copy)
                    last.then_inc(v_made, 1)
                if name == "transpose":
                    sc.wait_ge(transposed, pair + 1)
                    nc.scalar.activation(q_t[:, :, :], bank["queries"].rearrange("p (c t) -> p c t", t=128),
                                         ACT.Copy).then_inc(q_copied, 1)
                if name in ("score", "score2"):
                    for half in (0,) if name == "score" else (1,):
                        part = slice(8 * half, 8 * half + 8)
                        sc.wait_ge(shifted, 2 * pair + half + 1)
                        nc.scalar.activation(probs[:, part, :], probs[:, part, :], ACT.Exp,
                                             scale=HD ** -0.5).then_inc(probs_made, 1)
                if name == "turn":
                    sc.wait_ge(probs_turned, 2 * pair + 1)
                    nc.scalar.activation(p_t[:, 0:4, :], bank["turned"][0].rearrange("p (j t) -> p j t", t=128),
                                         ACT.Copy).then_inc(pt_x_copied, 1)
                if name == "project":
                    sc.wait_ge(x2_turned, pair + 1)
                    nc.scalar.activation(x2t[:, :, :],
                                         bank["x2"][:, 0:D].rearrange("p (c t) -> p c t", t=128),
                                         ACT.Copy)
                    nc.scalar.activation(x2t_hi[:, par, :, p * PAIR:(p + 1) * PAIR],
                                         bank["x2"][:, 0:D].rearrange("p (c t) -> p c t", t=128),
                                         ACT.Copy).then_inc(x2t_hi_made, 1)
                if name == "route":
                    sc.wait_ge(route_step, 4 * pair + 4)
                    nc.scalar.activation(exped[:, :], exponent[:, :], ACT.Exp).then_inc(exps_made, 1)

            def make_hi(n, slot, rows):
                after(sc, weighted, n + 1)
                after(sc, down_done, n - 1)
                nc.scalar.activation(h_hi[rows, slot, :], act[rows, slot, :], ACT.Copy)\
                    .then_inc(hi_ready, 1)

            def weights_hi(i):
                slot = i % STAGING
                sc.wait_ge(raw_loaded[slot], 48 * (i // STAGING + 1))
                n = 128 if i < CHUNKS - 1 else SHARED_REST
                if n < 128:
                    sc.wait_ge(const_made, CONSTS)
                width = 2 * KC * n
                nc.scalar.activation(wgu_hi[:, i, 0:width], raw[:, slot, 0:width], ACT.Copy)
                nc.scalar.activation(wd_hi[0:n, i, :], raw[0:n, slot, 2 * D:3 * D], ACT.Copy)\
                    .then_inc(w_hi_made, 1)

            def body(ffn, par, att):
                first = isinstance(ffn, int) and ffn == 0
                for k, (early, late) in enumerate(steps_by_point("ACT", ffn is None)):
                    if att is not None:
                        for name, p in early:
                            attention(name, p, att, 0 if ffn is None else 1 - par, ffn is None)
                    i = k // 2
                    if ffn is None and k == 2:
                        gates_tanh()
                    for chunk in weights_at(k, ffn):
                        weights_hi(chunk)
                    if ffn is not None and k % 2 == 0:
                        n = CHUNKS * ffn + i
                        after(sc, lo_ready, n - 1)
                        after(sc, gate_ready, n + 1)
                        rows = rows_of(i)
                        nc.scalar.activation(act[rows, i % 2, :], gate_ps[i % 2][rows, :], ACT.Tanh,
                                             scale=0.5).then_inc(tanh_ready, 1)
                    if ffn is not None and k % 2 == 1 and not (first and i == 0):
                        make_hi(CHUNKS * ffn + i - 1, (i - 1) % 2, rows_of((i - 1) % CHUNKS))
                    if att is not None:
                        for name, p in late:
                            attention(name, p, att, 0 if ffn is None else 1 - par, ffn is None)

            run(sc, lambda: None, body, lambda: make_hi(
                CHUNKS * groups - 1, (CHUNKS - 1) % 2, rows_of(CHUNKS - 1)))

        @block.vector
        def _(ve):
            def prepare():
                ve.wait_ge(const_made, 1)

            def attention(name, p, group, par, alone):
                pair = PAIRS * group + p
                bank, p_t = att_banks(alone), p_t_of[alone]
                if name == "norm":
                    src = x_in[:, p, :]
                    after(ve, x_loaded[p], 16 * (group + 1))
                    nc.vector.bn_stats(stats[:, :], src).then_inc(norm1_step, 1)
                    after(ve, norm1_step, 3 * pair + 1, APART)
                    nc.vector.bn_aggr(moments[:, :], stats[:, :]).then_inc(norm1_step, 1)
                    after(ve, norm1_step, 3 * pair + 2)
                    nc.vector.tensor_scalar(rstd[:, :], moments[:, 1:2], EPS, None, ALU.add)\
                        .then_inc(norm1_step, 1)
                if name == "center":
                    src = x_in[:, p, :]
                    after(ve, rstd1_made, pair + 1)
                    after(ve, transposed, pair)
                    for b in range(2):
                        rows = slice(b * SEQ, (b + 1) * SEQ)
                        last = nc.vector.tensor_scalar(
                            x_norm[rows, :, b, :], src[rows, :].rearrange("p (c n) -> p c n", c=QUARTERS),
                            moments[rows, 0:1], rstd[rows, :], ALU.subtract, ALU.mult)
                    last.then_inc(queries_normed, 1)
                if name == "transpose":
                    after(ve, transposed, pair + 1)
                    nc.vector.tensor_copy(k_t[:, :, :],
                                          bank["keys"][:, 0:QUARTERS * SEQ].rearrange("p (c k) -> p c k", k=SEQ))\
                        .then_inc(k_copied, 1)
                if name in ("score", "score2"):
                    mask = causal[:, :].unsqueeze(1).broadcast_to([128, HEADS // 2, SEQ])
                    if name == "score" and isinstance(group, int) and group == 0 and p == 0:
                        ve.wait_ge(const_made, CONSTS)
                    for half in (0,) if name == "score" else (1,):
                        part = slice(8 * half, 8 * half + 8)
                        if alone and half == 0:
                            after(ve, shifted, 2 * pair)
                        after(ve, scored, 2 * pair + half + 1, APART)
                        nc.vector.copy_predicated(
                            scores[:, part, :], mask,
                            bank["scores"][half].rearrange("p (h k) -> p h k", k=SEQ)).then_inc(masked, 1)
                        after(ve, masked, 2 * pair + half + 1)
                        nc.vector.tensor_reduce(row_max[:, part], scores[:, part, :], AX.X, ALU.max)\
                            .then_inc(maxed, 1)
                if name == "turn":
                    after(ve, probs_turned, 2 * pair + 2)
                    nc.vector.tensor_copy(p_t[:, 4:8, :],
                                          bank["turned"][1].rearrange("p (j t) -> p j t", t=128))\
                        .then_inc(pt_y_copied, 1)
                if name in ("value", "value2"):
                    for half in (0,) if name == "value" else (1,):
                        part = slice(8 * half, 8 * half + 8)
                        pv = bank["values"][half][:, 0:4 * VCOLS].rearrange("p (j v) -> p j v", v=VCOLS)
                        after(ve, valued, 2 * pair + half + 1)
                        nc.vector.reciprocal(inv_sum[:, part].rearrange("p (j h) -> p j h", h=2),
                                             pv[:, :, 4 * HD:VCOLS]).then_inc(inv_made, 1)
                        after(ve, inv_made, 2 * pair + half + 1)
                        for b in range(2):
                            rows = slice(b * SEQ, (b + 1) * SEQ)
                            last = nc.vector.tensor_tensor(
                                attended[rows, half * 128:(half + 1) * 128]
                                .rearrange("p (j h d) -> p j h d", j=4, h=2),
                                pv[rows, :, 2 * HD * b:2 * HD * (b + 1)]
                                .rearrange("p j (h d) -> p j h d", h=2),
                                inv_sum[rows, part].rearrange("p (j h) -> p j h", h=2)
                                .unsqueeze(3).broadcast_to([SEQ, 4, 2, HD]),
                                ALU.mult)
                if name == "value2":
                    last.then_inc(att_scaled, 1)
                    after(ve, att_scaled, pair + 1)
                    if isinstance(group, int) and group == 0:
                        ve.wait_ge(tanh_made, 1)
                    if p == 0:
                        after(ve, y_stored, 16 * PAIRS * (group - 1))
                    nc.vector.scalar_tensor_tensor(
                        out=x2[:, par, p, :], in0=attended[:, :], scalar=gate_tanh[:, 0:1],
                        in1=x_in[:, p, :], op0=ALU.mult, op1=ALU.add).then_inc(x2_made, 1)
                    after(ve, x2_made, pair + 1)
                    src = x2[:, par, p, :]
                    nc.vector.bn_stats(stats2[:, :], src).then_inc(norm2_step, 1)
                    after(ve, norm2_step, 3 * pair + 1, APART)
                    nc.vector.bn_aggr(moments2[:, :], stats2[:, :]).then_inc(norm2_step, 1)
                    after(ve, norm2_step, 3 * pair + 2)
                    nc.vector.tensor_scalar(rstd2[:, :], moments2[:, 1:2], EPS, None, ALU.add)\
                        .then_inc(norm2_step, 1)
                if name == "center2":
                    src = x2[:, par, p, :]
                    after(ve, rstd2_made, pair + 1)
                    if alone:
                        after(ve, x2_turned, pair)
                    nc.vector.tensor_scalar(x2_norm[:, :], src, moments2[:, 0:1], rstd2[:, :],
                                            ALU.subtract, ALU.mult).then_inc(x2_normed, 1)
                if name == "project":
                    after(ve, x2t_hi_made, pair + 1)
                    where = slice(p * PAIR, (p + 1) * PAIR)
                    nc.vector.tensor_tensor(x2t_lo[:, par, :, where],
                                            bank["x2"][:, 0:D].rearrange("p (c t) -> p c t", t=128),
                                            x2t_hi[:, par, :, where].bitcast(f32), ALU.subtract)\
                        .then_inc(x2t_lo_made, 1)
                if name == "route":
                    after(ve, routed, pair + 1)
                    nc.vector.tensor_copy(logits[:, 0:EXPERTS], bank["logits"][:, 0:EXPERTS])
                    nc.vector.tensor_scalar(exponent[:, EXPERTS:COMBINE], bank["logits"][:, EXPERTS:COMBINE],
                                            -1.0, None, ALU.mult).then_inc(logits_copied, 1)
                    after(ve, logits_copied, pair + 1, APART)
                    nc.vector.max(top8[:, :], logits[:, 0:EXPERTS]).then_inc(route_step, 1)
                    after(ve, route_step, 4 * pair + 1)
                    nc.vector.tensor_copy(top_k[:, 0:TOP_K], top8[:, 0:TOP_K]).then_inc(route_step, 1)
                if name == "choose":
                    after(ve, route_step, 4 * pair + 2, APART)
                    nc.vector.match_replace(replaced[:, :], top_k[:, :], logits[:, :], -FAR)\
                        .then_inc(route_step, 1)
                    nc.vector.tensor_scalar(exponent[:, 0:EXPERTS], logits[:, 0:EXPERTS], top8[:, 0:1],
                                            None, ALU.subtract).then_inc(route_step, 1)
                    after(ve, route_step, 4 * pair + 4)
                    nc.vector.tensor_tensor(chosen[:, :], replaced[:, 0:EXPERTS], logits[:, 0:EXPERTS],
                                            ALU.not_equal).then_inc(combined, 1)
                if name == "combine":
                    after(ve, combined, 6 * pair + 1)
                    after(ve, exps_made, pair + 1)
                    nc.vector.scalar_tensor_tensor(
                        out=weighed[:, :], in0=exped[:, 0:EXPERTS], scalar=1.0, in1=chosen[:, :],
                        op0=ALU.mult, op1=ALU.mult, accum_out=sums[:, 0:1]).then_inc(combined, 1)
                    nc.vector.tensor_scalar(sums[:, 1:2], exped[:, EXPERTS:COMBINE], 1.0, None, ALU.add)\
                        .then_inc(combined, 1)
                    after(ve, combined, 6 * pair + 3)
                    nc.vector.reciprocal(inv_sums[:, :], sums[:, :]).then_inc(combined, 1)
                    after(ve, combined, 6 * pair + 4)
                    if alone:
                        after(ve, combine_turned, pair)
                    nc.vector.tensor_scalar(combine[:, 0:EXPERTS], weighed[:, :], inv_sums[:, 0:1], 0.5,
                                            ALU.mult, ALU.mult).then_inc(combined, 1)
                    nc.vector.tensor_scalar(combine[:, EXPERTS:COMBINE], inv_sums[:, 1:2], 0.5, None,
                                            ALU.mult).then_inc(combined, 1)
                if name == "weigh":
                    after(ve, combine_turned, pair + 1)
                    after(ve, combine_stored, 16 * pair)
                    nc.vector.tensor_copy(combine_t[:, :], bank["combine"][0:COMBINE, 0:128])\
                        .then_inc(combine_t_copied, 1)

            def weights_lo(i):
                slot = i % STAGING
                ve.wait_ge(w_hi_made, i + 1)
                n = 128 if i < CHUNKS - 1 else SHARED_REST
                width = 2 * KC * n
                nc.vector.tensor_tensor(wgu_lo[:, i, 0:width], raw[:, slot, 0:width],
                                        wgu_hi[:, i, 0:width].bitcast(f32), ALU.subtract)
                nc.vector.tensor_tensor(wd_lo[0:n, i, :], raw[0:n, slot, 2 * D:3 * D],
                                        wd_hi[0:n, i, :].bitcast(f32), ALU.subtract)\
                    .then_inc(w_lo_made, 1)

            def split_lo(n, slot, rows):
                after(ve, hi_ready, n + 1)
                nc.vector.tensor_tensor(h_lo[rows, slot, :], act[rows, slot, :],
                                        h_hi[rows, slot, :].bitcast(f32), ALU.subtract)\
                    .then_inc(lo_ready, 1)

            def finish_group(group, par):
                after(ve, down_done, CHUNKS * (group + 1))
                for p in range(PAIRS):
                    nc.vector.scalar_tensor_tensor(
                        out=x2[:, par, p, :], in0=out_ps[:, p, :], scalar=gate_tanh[:, 1:2],
                        in1=x2[:, par, p, :], op0=ALU.mult, op1=ALU.add).then_inc(y_ready, 1)

            def body(ffn, par, att):
                first = isinstance(ffn, int) and ffn == 0
                for k, (early, late) in enumerate(steps_by_point("DVE", ffn is None)):
                    n = None if ffn is None else CHUNKS * ffn + k // 2
                    if k == 4 and ffn is not None and not first:
                        finish_group(ffn - 1, 1 - par)
                    if att is not None:
                        for name, p in early:
                            attention(name, p, att, 0 if ffn is None else 1 - par, ffn is None)
                    i = k // 2
                    if ffn is not None and k % 2 == 1 and not (first and i == 0):
                        split_lo(n - 1, (i - 1) % 2, rows_of((i - 1) % CHUNKS))
                    for chunk in weights_at(k, ffn):
                        weights_lo(chunk)
                    if ffn is not None and k % 2 == 0:
                        rows = rows_of(i)
                        a, gate, up = act[rows, i % 2, :], gate_ps[i % 2][rows, :], up_ps[i % 2][rows, :]
                        after(ve, tanh_ready, n + 1)
                        nc.vector.scalar_tensor_tensor(out=a, in0=a, scalar=1.0, in1=gate,
                                                       op0=ALU.add, op1=ALU.mult).then_inc(gated, 1)
                        if i < CHUNKS - 1:
                            after(ve, up_ready, (CHUNKS - 1) * ffn + i + 1)
                        else:
                            up = gate_ps[i % 2][SHARED_REST:2 * SHARED_REST, :]
                        after(ve, gated, n + 1)
                        nc.vector.tensor_tensor(a, a, up, ALU.mult).then_inc(upped, 1)
                    if att is not None:
                        for name, p in late:
                            attention(name, p, att, 0 if ffn is None else 1 - par, ffn is None)

            def drain():
                split_lo(CHUNKS * groups - 1, (CHUNKS - 1) % 2, rows_of(CHUNKS - 1))
                finish_group(groups - 1, (groups - 1) % 2)

            run(ve, prepare, body, drain)

        @block.tensor
        def _(te):
            def three(out_ap, a_hi, a_lo, b_hi, b_lo, first, last, check=False):
                nc.tensor.matmul(out_ap, a_hi, b_hi, start=first, stop=False, skip_group_check=check)
                nc.tensor.matmul(out_ap, a_hi, b_lo, start=False, stop=False, skip_group_check=check)
                return nc.tensor.matmul(out_ap, a_lo, b_hi, start=False, stop=last,
                                        skip_group_check=check)

            def attention(name, p, group, par, alone):
                pair = PAIRS * group + p
                bank, p_t = att_banks(alone), p_t_of[alone]
                if name == "transpose":
                    after(te, queries_normed, pair + 1)
                    after(te, ctx_loaded, 64 * (pair + 1))
                    if alone:
                        after(te, q_copied, pair)
                        after(te, k_copied, pair)
                    elif p:
                        after(te, att_scaled, pair)
                        after(te, combine_t_copied, pair - 1)
                    else:
                        after(te, x2t_lo_made, pair)
                        after(te, combine_t_copied, pair)
                    for c in range(QUARTERS):
                        nc.tensor.transpose(bank["queries"][:, c * 128:(c + 1) * 128],
                                            x_norm[:, c, :, :].rearrange("p b n -> p (b n)"), ident[:, :])
                    for c in range(QUARTERS):
                        last = nc.tensor.transpose(bank["keys"][:, c * SEQ:(c + 1) * SEQ],
                                                   ctx_k[0:SEQ, c, :, :].rearrange("p b n -> p (b n)"),
                                                   ident[0:SEQ, 0:SEQ])
                    last.then_inc(transposed, 1)
                if name == "score":
                    after(te, q_copied, pair + 1)
                    if not alone:
                        after(te, x2t_lo_made, pair if p else 0)
                    for half in range(2):
                        after(te, k_expanded, 2 * pair + half + 1)
                        if alone:
                            after(te, masked, 2 * pair - 1 + half)
                        for c in (2 * half, 2 * half + 1):
                            last = nc.tensor.matmul(
                                bank["scores"][half][:, (c % 2) * 256:(c % 2 + 1) * 256], q_t[:, c, :],
                                k_block[:, c, :, :].rearrange("p h k -> p (h k)"), start=True,
                                stop=True)
                        last.then_inc(scored, 1)
                if name == "turn":
                    if not alone:
                        after(te, logits_copied, pair if p else 0)
                    for half, copied in enumerate((pt_x_copied, pt_y_copied)):
                        after(te, probs_made, 2 * pair + half + 1)
                        if alone:
                            after(te, copied, pair)
                        for j in range(4 * half, 4 * half + 4):
                            last = nc.tensor.transpose(
                                bank["turned"][half][:, (j % 4) * 128:(j % 4 + 1) * 128],
                                probs[:, 2 * j:2 * j + 2, :].rearrange("p h k -> p (h k)"), ident[:, :])
                        last.then_inc(probs_turned, 1)
                if name == "value":
                    after(te, v_made, pair + 1)
                    if alone:
                        after(te, att_scaled, pair)
                    for half, copied in enumerate((pt_x_copied, pt_y_copied)):
                        after(te, copied, pair + 1)
                        for j in range(4 * half, 4 * half + 4):
                            last = nc.tensor.matmul(
                                bank["values"][half][:, (j % 4) * VCOLS:(j % 4 + 1) * VCOLS],
                                p_t[:, j, :], v_block[:, j, :], start=True, stop=True)
                        last.then_inc(valued, 1)
                if name == "project":
                    after(te, x2_normed, pair + 1)
                    if alone:
                        after(te, x2t_lo_made, pair)
                    elif p < PAIRS - 1:
                        after(te, q_copied, pair + 2)
                    for c in range(KC):
                        last = nc.tensor.transpose(bank["x2"][:, c * 128:(c + 1) * 128],
                                                   x2_norm[:, c * 128:(c + 1) * 128], ident[:, :])
                    last.then_inc(x2_turned, 1)
                if name == "route":
                    after(te, x2t_hi_made, pair + 1)
                    if isinstance(group, int) and group == 0 and p == 0:
                        te.wait_ge(small_loaded, 16 * (2 * KC + 2))
                    if alone:
                        after(te, logits_copied, pair)
                    elif p < PAIRS - 1:
                        after(te, masked, 2 * (pair + 2))
                    for c in range(KC):
                        last = nc.tensor.matmul(bank["logits"][:, 0:COMBINE], x2t[:, c, :],
                                                w_route[:, c, :], start=c == 0, stop=c == KC - 1)
                    last.then_inc(routed, 1)
                if name == "weigh":
                    after(te, combined, 6 * (pair + 1))
                    if alone:
                        after(te, combine_t_copied, pair)
                    elif p < PAIRS - 1:
                        after(te, att_scaled, pair + 2)
                    nc.tensor.transpose(bank["combine"][0:COMBINE, 0:128], combine[:, :], ident[:, :])\
                        .then_inc(combine_turned, 1)

            def gate_up(group, par, i):
                n = CHUNKS * group + i
                after(te, upped if i == 1 else gated, n - 1)
                if isinstance(group, int) and group == 0:
                    te.wait_ge(w_lo_made, i + 1)
                if i == 0:
                    after(te, x2t_lo_made, PAIRS * (group + 1))
                hi, lo = gate_up_of(wgu_hi[:, i, :], i), gate_up_of(wgu_lo[:, i, :], i)
                if i == CHUNKS - 1:
                    after(te, upped, n - 1)
                    for c in range(KC):
                        last = three(gate_ps[i % 2][:, :], hi[:, c, :, :].rearrange("p s f -> p (s f)"),
                                     lo[:, c, :, :].rearrange("p s f -> p (s f)"),
                                     x2t_hi[:, par, c, :], x2t_lo[:, par, c, :], c == 0, c == KC - 1)
                    last.then_inc(gate_ready, 1)
                    return
                for s, bank, ready in ((0, gate_ps, gate_ready), (1, up_ps, up_ready)):
                    if s:
                        after(te, upped, n - 1)
                    for c in range(KC):
                        last = three(bank[i % 2][:, :], hi[:, c, s, :], lo[:, c, s, :],
                                     x2t_hi[:, par, c, :], x2t_lo[:, par, c, :], c == 0, c == KC - 1)
                    last.then_inc(ready, 1)

            def down(group, i):
                n = CHUNKS * group + i
                after(te, lo_ready, n + 1)
                if i == 0:
                    after(te, y_ready, PAIRS * group)
                for p in range(PAIRS):
                    where = slice(p * PAIR, (p + 1) * PAIR)
                    last = three(out_ps[:, p, :], h_hi[:, i % 2, where], h_lo[:, i % 2, where],
                                 wd_hi[:, i, :], wd_lo[:, i, :], i == 0 and p % 2 == 0,
                                 i == CHUNKS - 1, True)
                last.then_inc(down_done, 1)

            def prepare():
                te.wait_ge(const_made, 2)

            def body(ffn, par, att):
                first = isinstance(ffn, int) and ffn == 0
                for k, (early, late) in enumerate(steps_by_point("PE", ffn is None)):
                    if att is not None:
                        for name, p in early:
                            attention(name, p, att, 0 if ffn is None else 1 - par, ffn is None)
                    i = k // 2
                    if ffn is not None and k % 2 == 0:
                        gate_up(ffn, par, i)
                    if ffn is not None and k % 2 == 1:
                        if i >= 2:
                            down(ffn, i - 2)
                        elif not first:
                            down(ffn - 1, CHUNKS + i - 2)
                    if att is not None:
                        for name, p in late:
                            attention(name, p, att, 0 if ffn is None else 1 - par, ffn is None)

            def drain():
                down(groups - 1, CHUNKS - 2)
                down(groups - 1, CHUNKS - 1)

            run(te, prepare, body, drain)


_INS = ["x", "ctx_2048", "g_xattn", "g_ffn", "L0_ffn_w_router", "L0_ffn_w_gate", "L0_ffn_w_up",
        "L0_ffn_w_down", "L0_ffn_w_sh_gate", "L0_ffn_w_sh_up", "L0_ffn_w_sh_down",
        "L0_ffn_w_sh_expert_gate"]


def kernel(**inputs):
    import numpy as _np
    import concourse.bacc as _bacc
    from concourse import mybir as _mybir
    from concourse.bass_utils import run_bass_kernel_spmd as _run

    nc = _bacc.Bacc("TRN2", target_bir_lowering=False, num_devices=1, dynamic_dma_scratch_size=1024)
    arrays, args = {}, []
    for name in _INS:
        a = _np.ascontiguousarray(inputs[name])
        arrays[f"in_{name}"] = a
        args.append(nc.dram_tensor(f"in_{name}", a.shape, _mybir.dt.from_np(a.dtype),
                                   kind="ExternalInput").ap())
    shape = inputs["x"].shape
    args.append(nc.dram_tensor("out_0", shape, _mybir.dt.float32, kind="ExternalOutput").ap())
    flamingo_block(nc, *args)
    r = _run(nc, [arrays], core_ids=[0])
    return r.results[0]["out_0"]
```
